# Optimizing a Trainium2 kernel written in Bass

```python
import numpy as np
import jax
import jax.numpy as jnp

def _softmax(x, axis=-1):
    return jax.nn.softmax(x, axis=axis)

def _gelu(x):
    return jax.nn.gelu(x, approximate=True)

def _silu(x):
    return jax.nn.silu(x)

def _sigmoid(x):
    return jax.nn.sigmoid(x)

def _layernorm(x, axis=-1, eps=1e-05):
    m = jnp.mean(x, axis=axis, keepdims=True)
    v = jnp.var(x, axis=axis, keepdims=True)
    return (x - m) / jnp.sqrt(v + eps)

def _scatter_add(tgt, idx, src, axis=0):
    return tgt.at[idx].add(src)

def _segment_sum(src, seg, n):
    return jax.ops.segment_sum(src, seg, n)
kernel_name = 'mk_dlrm_tower_d1_rec_r8_fc21fe'

def setup_inputs(seed: int=0):
    np.random.seed(seed)
    _w = jnp.asarray

    def _rec_inputs():
        import jax
        import jax.numpy as jnp
        _tk = jax.random.key(seed)
        dense_ctx = jax.random.normal(jax.random.fold_in(_tk, 190), (2048, 16), jnp.float32)
        ids = jnp.stack([jax.random.randint(jax.random.fold_in(_tk, 200 + f), (2048,), 0, v, jnp.int32) for f, v in enumerate([1250, 1250, 1250, 1250, 125000, 125000, 125000, 1250, 1250, 1250, 12500, 1250, 12500, 1000, 1000, 1000, 12500, 1250, 1250, 1250, 12500, 12500, 1250, 1000, 1000, 1250, 1000, 1250, 12500, 1000, 1000, 1000])], axis=1)
        tbl_0 = 0.05 * jax.random.normal(jax.random.fold_in(_tk, 500 + 0), (1250, 64), jnp.float32)
        tbl_1 = 0.05 * jax.random.normal(jax.random.fold_in(_tk, 500 + 1), (1250, 64), jnp.float32)
        tbl_2 = 0.05 * jax.random.normal(jax.random.fold_in(_tk, 500 + 2), (1250, 64), jnp.float32)
        tbl_3 = 0.05 * jax.random.normal(jax.random.fold_in(_tk, 500 + 3), (1250, 64), jnp.float32)
        tbl_4 = 0.05 * jax.random.normal(jax.random.fold_in(_tk, 500 + 4), (125000, 64), jnp.float32)
        tbl_5 = 0.05 * jax.random.normal(jax.random.fold_in(_tk, 500 + 5), (125000, 64), jnp.float32)
        tbl_6 = 0.05 * jax.random.normal(jax.random.fold_in(_tk, 500 + 6), (125000, 64), jnp.float32)
        tbl_7 = 0.05 * jax.random.normal(jax.random.fold_in(_tk, 500 + 7), (1250, 64), jnp.float32)
        tbl_8 = 0.05 * jax.random.normal(jax.random.fold_in(_tk, 500 + 8), (1250, 64), jnp.float32)
        tbl_9 = 0.05 * jax.random.normal(jax.random.fold_in(_tk, 500 + 9), (1250, 64), jnp.float32)
        tbl_10 = 0.05 * jax.random.normal(jax.random.fold_in(_tk, 500 + 10), (12500, 64), jnp.float32)
        tbl_11 = 0.05 * jax.random.normal(jax.random.fold_in(_tk, 500 + 11), (1250, 64), jnp.float32)
        tbl_12 = 0.05 * jax.random.normal(jax.random.fold_in(_tk, 500 + 12), (12500, 64), jnp.float32)
        tbl_13 = 0.05 * jax.random.normal(jax.random.fold_in(_tk, 500 + 13), (1000, 64), jnp.float32)
        tbl_14 = 0.05 * jax.random.normal(jax.random.fold_in(_tk, 500 + 14), (1000, 64), jnp.float32)
        tbl_15 = 0.05 * jax.random.normal(jax.random.fold_in(_tk, 500 + 15), (1000, 64), jnp.float32)
        tbl_16 = 0.05 * jax.random.normal(jax.random.fold_in(_tk, 500 + 16), (12500, 64), jnp.float32)
        tbl_17 = 0.05 * jax.random.normal(jax.random.fold_in(_tk, 500 + 17), (1250, 64), jnp.float32)
        tbl_18 = 0.05 * jax.random.normal(jax.random.fold_in(_tk, 500 + 18), (1250, 64), jnp.float32)
        tbl_19 = 0.05 * jax.random.normal(jax.random.fold_in(_tk, 500 + 19), (1250, 64), jnp.float32)
        tbl_20 = 0.05 * jax.random.normal(jax.random.fold_in(_tk, 500 + 20), (12500, 64), jnp.float32)
        tbl_21 = 0.05 * jax.random.normal(jax.random.fold_in(_tk, 500 + 21), (12500, 64), jnp.float32)
        tbl_22 = 0.05 * jax.random.normal(jax.random.fold_in(_tk, 500 + 22), (1250, 64), jnp.float32)
        tbl_23 = 0.05 * jax.random.normal(jax.random.fold_in(_tk, 500 + 23), (1000, 64), jnp.float32)
        tbl_24 = 0.05 * jax.random.normal(jax.random.fold_in(_tk, 500 + 24), (1000, 64), jnp.float32)
        tbl_25 = 0.05 * jax.random.normal(jax.random.fold_in(_tk, 500 + 25), (1250, 64), jnp.float32)
        tbl_26 = 0.05 * jax.random.normal(jax.random.fold_in(_tk, 500 + 26), (1000, 64), jnp.float32)
        tbl_27 = 0.05 * jax.random.normal(jax.random.fold_in(_tk, 500 + 27), (1250, 64), jnp.float32)
        tbl_28 = 0.05 * jax.random.normal(jax.random.fold_in(_tk, 500 + 28), (12500, 64), jnp.float32)
        tbl_29 = 0.05 * jax.random.normal(jax.random.fold_in(_tk, 500 + 29), (1000, 64), jnp.float32)
        tbl_30 = 0.05 * jax.random.normal(jax.random.fold_in(_tk, 500 + 30), (1000, 64), jnp.float32)
        tbl_31 = 0.05 * jax.random.normal(jax.random.fold_in(_tk, 500 + 31), (1000, 64), jnp.float32)
        _rk = jax.random.fold_in(_tk, 7)
        W_top1 = 0.0441942 * jax.random.normal(jax.random.fold_in(_tk, 801), (512, 512), jnp.float32)
        W_top2 = 0.0441942 * jax.random.normal(jax.random.fold_in(_tk, 802), (512, 256), jnp.float32)
        W_top3 = 0.0625 * jax.random.normal(jax.random.fold_in(_tk, 803), (256, 1), jnp.float32)
        b_top1 = jnp.zeros((512,), jnp.float32)
        b_top2 = jnp.zeros((256,), jnp.float32)
        return (dense_ctx, ids, tbl_0, tbl_1, tbl_2, tbl_3, tbl_4, tbl_5, tbl_6, tbl_7, tbl_8, tbl_9, tbl_10, tbl_11, tbl_12, tbl_13, tbl_14, tbl_15, tbl_16, tbl_17, tbl_18, tbl_19, tbl_20, tbl_21, tbl_22, tbl_23, tbl_24, tbl_25, tbl_26, tbl_27, tbl_28, tbl_29, tbl_30, tbl_31, W_top1, b_top1, W_top2, b_top2, W_top3)
    dense_ctx, ids, tbl_0, tbl_1, tbl_2, tbl_3, tbl_4, tbl_5, tbl_6, tbl_7, tbl_8, tbl_9, tbl_10, tbl_11, tbl_12, tbl_13, tbl_14, tbl_15, tbl_16, tbl_17, tbl_18, tbl_19, tbl_20, tbl_21, tbl_22, tbl_23, tbl_24, tbl_25, tbl_26, tbl_27, tbl_28, tbl_29, tbl_30, tbl_31, W_top1, b_top1, W_top2, b_top2, W_top3 = _rec_inputs()

    def _L0_rec_setup():
        import jax, jax.numpy as jnp
        import numpy as np
        FIELDS = 32
        EMBED = 64
        BATCH = 1024
        PAIR = FIELDS * (FIELDS - 1) // 2

        def _pair_ids(fields):
            pairs = np.array([(i, j) for i in range(fields - 1) for j in range(i + 1, fields)], dtype=np.int32)
            return (jnp.asarray(pairs[:, 0]), jnp.asarray(pairs[:, 1]))
        key = jax.random.key(seed)
        k1, k2 = jax.random.split(key)
        inputs = jax.random.normal(k1, (BATCH, FIELDS, EMBED), dtype=jnp.float32)
        w = 0.05 * jax.random.normal(k2, (PAIR, EMBED, EMBED), dtype=jnp.float32)
        return {'inputs': inputs, 'w': w}
    _L0_rec_all = _L0_rec_setup()
    _L0_rec_in = {k: v for k, v in _L0_rec_all.items() if k in ('w',)}
    del _L0_rec_all
    return {'dense_ctx': dense_ctx, 'ids': ids, 'tbl_0': tbl_0, 'tbl_1': tbl_1, 'tbl_2': tbl_2, 'tbl_3': tbl_3, 'tbl_4': tbl_4, 'tbl_5': tbl_5, 'tbl_6': tbl_6, 'tbl_7': tbl_7, 'tbl_8': tbl_8, 'tbl_9': tbl_9, 'tbl_10': tbl_10, 'tbl_11': tbl_11, 'tbl_12': tbl_12, 'tbl_13': tbl_13, 'tbl_14': tbl_14, 'tbl_15': tbl_15, 'tbl_16': tbl_16, 'tbl_17': tbl_17, 'tbl_18': tbl_18, 'tbl_19': tbl_19, 'tbl_20': tbl_20, 'tbl_21': tbl_21, 'tbl_22': tbl_22, 'tbl_23': tbl_23, 'tbl_24': tbl_24, 'tbl_25': tbl_25, 'tbl_26': tbl_26, 'tbl_27': tbl_27, 'tbl_28': tbl_28, 'tbl_29': tbl_29, 'tbl_30': tbl_30, 'tbl_31': tbl_31, 'W_top1': W_top1, 'b_top1': b_top1, 'W_top2': W_top2, 'b_top2': b_top2, 'W_top3': W_top3, 'L0_rec_w': _L0_rec_in['w']}

def reference(dense_ctx, ids, tbl_0, tbl_1, tbl_2, tbl_3, tbl_4, tbl_5, tbl_6, tbl_7, tbl_8, tbl_9, tbl_10, tbl_11, tbl_12, tbl_13, tbl_14, tbl_15, tbl_16, tbl_17, tbl_18, tbl_19, tbl_20, tbl_21, tbl_22, tbl_23, tbl_24, tbl_25, tbl_26, tbl_27, tbl_28, tbl_29, tbl_30, tbl_31, W_top1, b_top1, W_top2, b_top2, W_top3, L0_rec_w):
    import jax
    import jax.numpy as jnp

    def _L0_rec_ref(inputs, w):
        import jax, jax.numpy as jnp
        import numpy as np
        FIELDS = 32
        EMBED = 64
        BATCH = 1024
        PAIR = FIELDS * (FIELDS - 1) // 2

        def _pair_ids(fields):
            pairs = np.array([(i, j) for i in range(fields - 1) for j in range(i + 1, fields)], dtype=np.int32)
            return (jnp.asarray(pairs[:, 0]), jnp.asarray(pairs[:, 1]))
        ids_x, ids_y = _pair_ids(FIELDS)
        p = inputs[:, ids_x, :]
        q = inputs[:, ids_y, :]
        pw = jnp.einsum('bpi,pij->bpj', p, w)
        out = jnp.einsum('bpj,bpj->bp', pw, q)
        return out
    e = jnp.stack([tbl_0[ids[:, 0]], tbl_1[ids[:, 1]], tbl_2[ids[:, 2]], tbl_3[ids[:, 3]], tbl_4[ids[:, 4]], tbl_5[ids[:, 5]], tbl_6[ids[:, 6]], tbl_7[ids[:, 7]], tbl_8[ids[:, 8]], tbl_9[ids[:, 9]], tbl_10[ids[:, 10]], tbl_11[ids[:, 11]], tbl_12[ids[:, 12]], tbl_13[ids[:, 13]], tbl_14[ids[:, 14]], tbl_15[ids[:, 15]], tbl_16[ids[:, 16]], tbl_17[ids[:, 17]], tbl_18[ids[:, 18]], tbl_19[ids[:, 19]], tbl_20[ids[:, 20]], tbl_21[ids[:, 21]], tbl_22[ids[:, 22]], tbl_23[ids[:, 23]], tbl_24[ids[:, 24]], tbl_25[ids[:, 25]], tbl_26[ids[:, 26]], tbl_27[ids[:, 27]], tbl_28[ids[:, 28]], tbl_29[ids[:, 29]], tbl_30[ids[:, 30]], tbl_31[ids[:, 31]]], axis=1)
    z = _L0_rec_ref(e, L0_rec_w)
    z = z.reshape(z.shape[0], -1)
    h = jnp.concatenate([z, dense_ctx], axis=1)
    h = jnp.maximum(h @ W_top1 + b_top1, 0.0)
    h = jnp.maximum(h @ W_top2 + b_top2, 0.0)
    y = h @ W_top3
    return y

_drawn_inputs = setup_inputs


def setup_inputs(seed=0):
    import zlib

    import numpy as np

    out = dict(_drawn_inputs(seed))
    spreads = {'b_top1': (0.0, 0.1), 'b_top2': (0.0, 0.1)}
    factors = {'tbl_0': 6.428,
     'tbl_1': 5.987,
     'tbl_2': 5.677,
     'tbl_3': 5.661,
     'tbl_4': 4.81,
     'tbl_5': 6.151,
     'tbl_6': 5.598,
     'tbl_7': 4.816,
     'tbl_8': 5.653,
     'tbl_9': 5.574,
     'tbl_10': 5.534,
     'tbl_11': 5.337,
     'tbl_12': 5.454,
     'tbl_13': 5.104,
     'tbl_14': 5.908,
     'tbl_15': 5.651,
     'tbl_16': 5.072,
     'tbl_17': 5.806,
     'tbl_18': 5.055,
     'tbl_19': 5.652,
     'tbl_20': 5.228,
     'tbl_21': 5.394,
     'tbl_22': 5.702,
     'tbl_23': 5.869,
     'tbl_24': 5.743,
     'tbl_25': 5.311,
     'tbl_26': 5.656,
     'tbl_27': 5.656,
     'tbl_28': 5.833,
     'tbl_29': 5.615,
     'tbl_30': 5.514,
     'tbl_31': 6.085}
    for name, (base, spread) in spreads.items():
        noise = np.random.default_rng([zlib.crc32(name.encode()), seed]).standard_normal(out[name].shape)
        drawn = base * np.exp(spread * noise) if base else spread * noise
        out[name] = jnp.asarray(drawn.astype(out[name].dtype))
    for name, factor in factors.items():
        out[name] = (out[name] * factor).astype(out[name].dtype)
    return out
```

```python
from contextlib import ExitStack

import concourse.bass as bass
import numpy as np
from concourse import mybir

FIELDS, EMBED, BATCH, DENSE = 32, 64, 2048, 16
H1, H2 = 512, 256
P = 128
TB = 512
TILES = BATCH // TB
BLOCKS = TB // P
TWINS = FIELDS // 2


def pair_row(i, j):
    return i * (2 * FIELDS - i - 1) // 2 + j - i - 1


def chunk_order():
    chunks = []
    for i in range(FIELDS - 2, -1, -1):
        chunks += [("twin", i, m) for m in range(i // 2 + 1, TWINS)]
        if i % 4 == 0:
            chunks.append(("odd", i, i // 4))
    return chunks


CHUNKS = chunk_order()
STEP = 4
STEPS = len(CHUNKS) // STEP
UNITS = len(CHUNKS) // 2
SLOTS = 32 // 2
ZBANKS = 4
TWIN_CHUNKS = [c for c in CHUNKS if c[0] == "twin"]
ODD = FIELDS // 4
WG = 8
WGROUPS = len(TWIN_CHUNKS) // WG
WCOLS = WG * P
MLP = H1 // P + H2 // P + 1


def chunk_pairs(chunk):
    kind, i, m = chunk
    if kind == "twin":
        return [(i, 2 * m), (i, 2 * m + 1)]
    return [(4 * m, 4 * m + 1), (4 * m + 2, 4 * m + 3)]


def z_row(c, half):
    bank, step, group = c // (STEP * SLOTS), c % (STEP * SLOTS) // STEP, c % STEP
    return bank * P + 32 * group + 2 * step + half


def dense_row(d):
    return (ZBANKS - 1) * P + 32 * (d // 4) + 28 + d % 4


def tile_schedule():
    group_end = {}
    seen = 0
    for c, chunk in enumerate(CHUNKS):
        if chunk[0] == "twin":
            seen += 1
            if seen % WG == 0:
                group_end[seen // WG - 1] = c // STEP
    ev = [("W", 0), ("W", 1), ("W", 2), ("D",), ("T", 0), ("T", 1), ("M", 0), ("T", 2), ("M", 1)]
    next_t, next_m = 3, 2
    for t in range(STEPS):
        lowest = min(i for _, i, _ in CHUNKS[STEP * t:STEP * t + STEP])
        while next_t < TWINS and lowest <= (35 if next_t <= 6 else 33) - 2 * next_t:
            ev.append(("T", next_t))
            next_t += 1
        ev.append(("S", t))
        ev += [("W", g + 3) for g in range(WGROUPS - 3) if group_end[g] == t]
        if next_m < MLP:
            ev.append(("M", next_m))
            next_m += 1
        if t and t % SLOTS == 0:
            ev.append(("Z", t // SLOTS - 1))
    return ev + [("R",), ("Z", ZBANKS - 1)]


SCHEDULE = tile_schedule()
TOWER = [("D",)] + [("M", n) for n in range(MLP)]
GATHER_RING, MOV_RING, W_RING, RAW_RING, PROD_RING = 8, 6, 4, 3, 4

CHUNK_OF_ODD = {m: c for c, (kind, _, m) in enumerate(CHUNKS) if kind == "odd"}
TWIN_INDEX = {c: n for n, c in enumerate(c for c, x in enumerate(CHUNKS) if x[0] == "twin")}


def last_unit_of_source(i):
    mine = [c for c, (kind, a, m) in enumerate(CHUNKS) if a == i or (kind == "odd" and i == 4 * m + 2)]
    return max(mine) // 2


def last_unit_of_group(g):
    return max(c for c, n in TWIN_INDEX.items() if n // WG == g) // 2


def mov_slot(i):
    return (FIELDS - 2 - i) % MOV_RING


def mov_uses(i):
    slot = mov_slot(i)
    per = len(range(slot, FIELDS - 1, MOV_RING))
    return per, (FIELDS - 2 - i) // MOV_RING + 1


def w_uses(g):
    return len(range(g % W_RING, WGROUPS, W_RING)), g // W_RING + 1


def tower_kernel(nc, ids, tables, dense, w_twin, w_odd, w1, b1, w2, b2, w3, out):
    fp32, f32r, i32 = mybir.dt.float32, mybir.dt.float32r, mybir.dt.int32
    ALU, ACT = mybir.AluOpType, mybir.ActivationFunctionType

    w_split = nc.dram_tensor("w_split", (WGROUPS, P, WCOLS), fp32, kind="Internal").ap()

    with ExitStack() as ctx:
        def sb(name, shape, dt=fp32):
            return ctx.enter_context(nc.sbuf_tensor(name, shape, dt))

        def ps(name, shape):
            return ctx.enter_context(nc.psum_tensor(name, shape, fp32))

        def sem(name):
            return ctx.enter_context(nc.semaphore(name))

        ids_sb = sb("ids_sb", [P, BLOCKS * FIELDS], i32)
        rows = sb("rows", [P, GATHER_RING, BLOCKS, P])
        vT = sb("vT", [P, TWINS, TB])
        v_odd = sb("v_odd", [P, 2, TB])
        halves = sb("halves", [P, 2, 2, TB], f32r)
        mov = sb("mov", [P, MOV_RING, 2, TB], f32r)
        w_raw = sb("w_raw", [P, RAW_RING, WCOLS])
        w_ring = sb("w_ring", [P, W_RING, WCOLS], f32r)
        w_odd_raw = sb("w_odd_raw", [P, ODD, 2, EMBED])
        w_odd_sb = sb("w_odd_sb", [P, ODD, 3, EMBED], f32r)
        prod = sb("prod", [P, PROD_RING, 2, TB])
        sel = sb("sel", [P, SLOTS, 32])
        ident = sb("ident", [P, P])
        z_sb = sb("z_sb", [P, ZBANKS, TB])
        h1_sb = sb("h1_sb", [P, H1 // P, TB])
        h2_sb = sb("h2_sb", [P, H2 // P, TB])
        y_sb = sb("y_sb", [1, TB])
        w1_sb = sb("w1_sb", [P, ZBANKS, H1])
        w2_sb = sb("w2_sb", [P, H1 // P, H2])
        w3_sb = sb("w3_sb", [P, H2 // P])
        b1_sb = sb("b1_sb", [P, H1 // P])
        b2_sb = sb("b2_sb", [P, H2 // P])

        proj = [ps(f"proj{n}", [P, 2, TB]) for n in range(2)]
        z_ps = [ps(f"z_ps{n}", [P, TB]) for n in range(2)]
        turn_ps = ps("turn_ps", [P, TB])
        mlp_ps = ps("mlp_ps", [P, TB])

        s_passed = sem("waits_passed")
        s_ids = sem("ids_loaded")
        s_rows = [sem(f"rows_gathered{n}") for n in range(GATHER_RING)]
        s_ident = sem("ident_made")
        s_sel = sem("sel_made")
        s_par = sem("parameters_loaded")
        s_oraw = sem("w_odd_loaded")
        s_ohi = sem("w_odd_hi")
        s_olo = sem("w_odd_split")
        s_raw = [sem(f"w_raw_loaded{n}") for n in range(RAW_RING)]
        s_whi = sem("w_hi")
        s_wsp = sem("w_split_done")
        s_scr = [sem(f"w_stored{n}") for n in range(W_RING)]
        s_w = [sem(f"w_loaded{n}") for n in range(W_RING)]
        s_turn = sem("turned")
        s_vt = sem("vt_written")
        s_hi = sem("e_hi")
        s_lo = sem("e_lo")
        s_mov = [sem(f"mov_loaded{n}") for n in range(MOV_RING)]
        s_vodd = [sem(f"v_odd_loaded{n}") for n in range(2)]
        s_proj = sem("projected")
        s_prod = sem("multiplied")
        s_red = sem("reduced")
        s_z = sem("z_copied")
        s_dense = sem("dense_loaded")
        s_tower = sem("tower_summed")
        s_act = sem("tower_activated")
        s_out = sem("out_stored")

        block = ctx.enter_context(nc.Block())

        def wait(eng, s, tile, per_tile, count):
            value = tile * per_tile + count
            if not isinstance(tile, int) or value > 0:
                eng.wait_ge(s, value)
            if not isinstance(tile, int) and eng in alone:
                eng.sem_inc(s_passed, 1)

        alone = []

        def over_tiles(eng, body):
            body(0)
            with eng.Fori(1, TILES) as tile:
                body(tile)

        @block.gpsimd
        def _(pool):
            alone.append(pool)
            pool.memset(ident[:, :], 0.0).then_inc(s_ident, 1)
            pool.wait_ge(s_ident, 1)
            pool.affine_select(out=ident[:, :], in_=ident[:, :], compare_op=ALU.not_equal, fill=1.0,
                               base=0, pattern=[[-1, P]], channel_multiplier=1).then_inc(s_ident, 1)

            def body(tile):
                for n in range(GATHER_RING):
                    wait(pool, s_rows[n], tile, 2 * 128, 0)
                pool.dma_start(ids_sb[:, :], ids[tile, :, :]).then_inc(s_ids, 16)
                wait(pool, s_ids, tile, 16, 16)
                for k in range(TWINS):
                    wait(pool, s_turn, tile, TWINS, k - GATHER_RING + 1)
                    for blk in range(BLOCKS):
                        for half in range(2):
                            field = 2 * (TWINS - 1 - k) + half
                            at = blk * FIELDS + field
                            pool.indirect_dma_start(
                                rows[:, k % GATHER_RING, blk, half * EMBED:(half + 1) * EMBED], None,
                                tables[field],
                                bass.IndirectOffsetOnAxis(ap=ids_sb[:, at:at + 1], axis=0),
                            ).then_inc(s_rows[k % GATHER_RING], 16)

            over_tiles(pool, body)

        @block.sync
        def _(sp):
            alone.append(sp)
            def load_raw(g):
                if g >= RAW_RING:
                    sp.wait_ge(s_wsp, g - RAW_RING + 1)
                for half in range(2):
                    sp.dma_start(w_raw[half * EMBED:(half + 1) * EMBED, g % RAW_RING, :],
                                 w_twin[g, :, :]).then_inc(s_raw[g % RAW_RING], 16)

            def store_split(g):
                sp.wait_ge(s_wsp, g + 1)
                sp.dma_start(w_split[g, :, :], w_ring[:, g % W_RING, :].bitcast(fp32)).then_inc(s_scr[g % W_RING], 16)

            def weights(tile, g):
                if isinstance(tile, int):
                    for n in ([0, 1] if g == 0 else [g + 1]):
                        if n < WGROUPS:
                            load_raw(n)
                    if g:
                        store_split(g - 1)
                    return
                before = g - W_RING if g >= W_RING else max(range(g % W_RING, WGROUPS, W_RING))
                wait(sp, s_proj, tile, UNITS, last_unit_of_group(before) + 1 - (UNITS if g < W_RING else 0))
                sp.wait_ge(s_scr[g % W_RING], 16 * w_uses(g)[1])
                sp.dma_start(w_ring[:, g % W_RING, :].bitcast(fp32), w_split[g, :, :]).then_inc(s_w[g % W_RING], 16)

            def sources(tile, k):
                m = TWINS - 1 - k
                wait(sp, s_lo, tile, TWINS, k + 1)
                for i in (2 * m + 1, 2 * m):
                    if i == FIELDS - 1:
                        continue
                    before = i + MOV_RING
                    if before <= FIELDS - 2:
                        wait(sp, s_proj, tile, UNITS, last_unit_of_source(before) + 1)
                    else:
                        before = min(x for x in range(FIELDS - 1) if mov_slot(x) == mov_slot(i))
                        wait(sp, s_proj, tile, UNITS, last_unit_of_source(before) + 1 - UNITS)
                    src = halves[(i % 2) * EMBED:(i % 2 + 1) * EMBED, k % 2, :, :].bitcast(fp32)
                    for half in range(2):
                        sp.dma_start(mov[half * EMBED:(half + 1) * EMBED, mov_slot(i), :, :].bitcast(fp32),
                                     src).then_inc(s_mov[mov_slot(i)], 16)
                if m % 2 == 0:
                    g = m // 2
                    wait(sp, s_vt, tile, TWINS, k + 1)
                    if g + 2 < ODD:
                        wait(sp, s_prod, tile, UNITS, CHUNK_OF_ODD[g + 2] // 2 + 1)
                    else:
                        wait(sp, s_prod, tile, UNITS, CHUNK_OF_ODD[g % 2] // 2 + 1 - UNITS)
                    for half in range(2):
                        sp.dma_start(v_odd[half * EMBED:(half + 1) * EMBED, g % 2, :],
                                     vT[EMBED:P, m + half, :]).then_inc(s_vodd[g % 2], 16)

            def dense_rows(tile):
                wait(sp, s_z, tile, ZBANKS, 0)
                for q in range(4):
                    sp.dma_start(z_sb[32 * q + 28:32 * q + 32, ZBANKS - 1, :],
                                 dense[tile - 1, 4 * q:4 * q + 4, :]).then_inc(s_dense, 16)

            def result(tile):
                wait(sp, s_act, tile, MLP, 1)
                sp.dma_start(out[tile - 1, :, :], y_sb[:, :]).then_inc(s_out, 16)

            def body(tile):
                first = isinstance(tile, int)
                for ev in SCHEDULE:
                    if ev[0] == "W":
                        weights(tile, ev[1])
                    elif ev[0] == "T":
                        sources(tile, ev[1])
                    elif ev[0] == "D" and not first:
                        dense_rows(tile)
                    elif ev == ("M", MLP - 1) and not first:
                        result(tile)
                if first:
                    store_split(WGROUPS - 1)

            over_tiles(sp, body)
            dense_rows(TILES)
            result(TILES)
            sp.wait_ge(s_out, 16 * TILES + 16)

        @block.scalar
        def _(act):
            for half in range(2):
                act.dma_start(w_odd_raw[half * EMBED:(half + 1) * EMBED, :, :, :], w_odd).then_inc(s_oraw, 16)
            act.dma_start(w1_sb[:, :, :], w1).then_inc(s_par, 16)
            act.dma_start(w2_sb[:, :, :], w2).then_inc(s_par, 16)
            act.dma_start(w3_sb[:, :], w3).then_inc(s_par, 16)
            act.dma_start(b1_sb[:, :], b1).then_inc(s_par, 16)
            act.dma_start(b2_sb[:, :], b2).then_inc(s_par, 16)
            act.sem_inc(s_act, 1)
            act.sem_inc(s_out, 16)
            act.wait_ge(s_oraw, 32)
            act.wait_ge(s_ohi, 1)
            act.activation(w_odd_sb[:, :, 0:3:2, :], w_odd_raw[:, :, :, :], ACT.Copy).then_inc(s_ohi, 1)
            act.wait_ge(s_par, 80)

            def weights_hi(g):
                act.wait_ge(s_raw[g % RAW_RING], 32 * (g // RAW_RING + 1))
                if g >= W_RING:
                    act.wait_ge(s_proj, last_unit_of_group(g - W_RING) + 1)
                    act.wait_ge(s_scr[g % W_RING], 16 * (g // W_RING))
                act.activation(w_ring[:, g % W_RING, :], w_raw[:, g % RAW_RING, :], ACT.Copy).then_inc(s_whi, 1)

            def turned(tile, k):
                m = TWINS - 1 - k
                wait(act, s_turn, tile, TWINS, k + 1)
                if k == 0:
                    wait(act, s_prod, tile, UNITS, 0)
                act.activation(vT[:, m, :], turn_ps[:, :], ACT.Copy).then_inc(s_vt, 1)
                before = m + 2 if k >= 2 else 1 - k
                for i in (2 * before, 2 * before + 1):
                    if i < FIELDS - 1:
                        per, use = mov_uses(i)
                        wait(act, s_mov[mov_slot(i)], tile, 32 * per, 32 * (use if k >= 2 else use - per))
                act.activation(halves[:, k % 2, 0, :], turn_ps[:, :], ACT.Copy).then_inc(s_hi, 1)

            def tower(tile, n):
                wait(act, s_tower, tile, MLP, n + 1 - MLP)
                if n < H1 // P:
                    act.activation(h1_sb[:, n, :], mlp_ps[:, :], ACT.Relu,
                                   bias=b1_sb[:, n:n + 1]).then_inc(s_act, 1)
                elif n < MLP - 1:
                    c = n - H1 // P
                    act.activation(h2_sb[:, c, :], mlp_ps[:, :], ACT.Relu,
                                   bias=b2_sb[:, c:c + 1]).then_inc(s_act, 1)
                else:
                    wait(act, s_out, tile, 16, 0)
                    act.activation(y_sb[:, :], mlp_ps[0:1, :], ACT.Copy).then_inc(s_act, 1)

            def z_copy(tile, G):
                wait(act, s_red, tile, STEPS, min(SLOTS * (G + 1), STEPS))
                act.activation(z_sb[:, G, :], z_ps[G % 2][:, :], ACT.Copy).then_inc(s_z, 1)

            def body(tile):
                first = isinstance(tile, int)
                for ev in SCHEDULE:
                    if ev[0] == "W" and first:
                        weights_hi(ev[1])
                    elif ev[0] == "T":
                        turned(tile, ev[1])
                    elif ev[0] == "M" and not first:
                        tower(tile, ev[1])
                    elif ev[0] == "Z":
                        z_copy(tile, ev[1])

            over_tiles(act, body)
            for n in range(MLP):
                tower(TILES, n)

        @block.vector
        def _(dve):
            dve.memset(w_odd_sb[:, :, :, :].bitcast(fp32), 0.0).then_inc(s_ohi, 1)
            dve.memset(sel[:, :, :], 0.0).then_inc(s_sel, 1)
            dve.wait_ge(s_sel, 1)
            flat = sel[:, :, :].rearrange("p s c -> p (s c)")
            for half in range(2):
                last = 34 * (SLOTS - 1) + half
                dve.memset(flat[half * EMBED:(half + 1) * EMBED, half:last + 1:34], 1.0).then_inc(s_sel, 1)
            dve.wait_ge(s_ohi, 2)
            dve.tensor_tensor(w_odd_sb[EMBED:P, :, 0:3:2, :], w_odd_raw[EMBED:P, :, :, :],
                              w_odd_sb[EMBED:P, :, 0:3:2, :].bitcast(fp32), ALU.subtract).then_inc(s_olo, 1)

            def weights_lo(g):
                dve.wait_ge(s_whi, g + 1)
                dve.tensor_tensor(w_ring[EMBED:P, g % W_RING, :], w_raw[EMBED:P, g % RAW_RING, :],
                                  w_ring[EMBED:P, g % W_RING, :].bitcast(fp32), ALU.subtract).then_inc(s_wsp, 1)

            def lo(tile, k):
                wait(dve, s_vt, tile, TWINS, k + 1)
                wait(dve, s_hi, tile, TWINS, k + 1)
                dve.tensor_tensor(halves[:, k % 2, 1, :], vT[:, TWINS - 1 - k, :],
                                  halves[:, k % 2, 0, :].bitcast(fp32), ALU.subtract).then_inc(s_lo, 1)

            def multiply(tile, u):
                a, b = CHUNKS[2 * u], CHUNKS[2 * u + 1]
                wait(dve, s_proj, tile, UNITS, u + 1)
                wait(dve, s_red, tile, STEPS, u // 2 + 1 - PROD_RING // 2)
                if a[0] == b[0] == "twin" and a[2] < b[2]:
                    dve.tensor_tensor(prod[:, u % PROD_RING, :, :], proj[u % 2][:, :, :],
                                      vT[:, a[2]:b[2] + 1:b[2] - a[2], :], ALU.mult).then_inc(s_prod, 1)
                    return
                for n, (kind, _, m) in enumerate((a, b)):
                    if kind == "odd":
                        wait(dve, s_vodd[m % 2], tile, 32 * ODD // 2, 32 * ((ODD - 1 - m) // 2 + 1))
                    target = vT[:, m, :] if kind == "twin" else v_odd[:, m % 2, :]
                    last = dve.tensor_tensor(prod[:, u % PROD_RING, n, :], proj[u % 2][:, n, :], target, ALU.mult)
                last.then_inc(s_prod, 1)

            def body(tile):
                first = isinstance(tile, int)
                for ev in SCHEDULE:
                    if ev[0] == "W" and first:
                        weights_lo(ev[1])
                    elif ev[0] == "T":
                        lo(tile, ev[1])
                    elif ev[0] == "S":
                        multiply(tile, 2 * ev[1])
                        multiply(tile, 2 * ev[1] + 1)

            over_tiles(dve, body)

        @block.tensor
        def _(pe):
            pe.wait_ge(s_ident, 2)
            pe.wait_ge(s_sel, 3)
            pe.wait_ge(s_olo, 1)

            def turn(tile, k):
                wait(pe, s_rows[k % GATHER_RING], tile, 2 * 128, 128 * (k // GATHER_RING + 1))
                wait(pe, s_hi, tile, TWINS, k)
                for blk in range(BLOCKS):
                    last = pe.transpose(turn_ps[:, blk * P:(blk + 1) * P],
                                        rows[:, k % GATHER_RING, blk, :], ident[:, :])
                last.then_inc(s_turn, 1)

            def weights_ready(tile, g):
                if isinstance(tile, int):
                    pe.wait_ge(s_wsp, g + 1)
                else:
                    per, use = w_uses(g)
                    wait(pe, s_w[g % W_RING], tile, 16 * per, 16 * (use - per))

            def source_ready(tile, i):
                per, use = mov_uses(i)
                wait(pe, s_mov[mov_slot(i)], tile, 32 * per, 32 * use)

            def project(tile, u):
                wait(pe, s_prod, tile, UNITS, u - 1)
                for n in range(2):
                    c = 2 * u + n
                    kind, i, m = CHUNKS[c]
                    if kind == "twin":
                        w = TWIN_INDEX[c]
                        if w % WG == 0:
                            weights_ready(tile, w // WG)
                        if m == i // 2 + 1:
                            source_ready(tile, i)
                        wt = w_ring[:, (w // WG) % W_RING, (w % WG) * P:(w % WG + 1) * P]
                        parts = [(wt, i)]
                    else:
                        if m == ODD - 1:
                            source_ready(tile, i + 2)
                        wo = w_odd_sb[:, m, :, :].rearrange("p a l -> p (a l)")
                        parts = [(wo[:, 0:P], i), (wo[:, EMBED:EMBED + P], i + 2)]
                    passes = [(wt, src, part) for wt, src in parts for part in range(2)]
                    for x, (wt, src, part) in enumerate(passes):
                        last = pe.matmul(proj[u % 2][:, n, :], lhsT=wt, rhs=mov[:, mov_slot(src), part, :],
                                         start=(x == 0), stop=(x == len(passes) - 1))
                last.then_inc(s_proj, 1)

            def reduce(tile, t):
                bank, slot = t // SLOTS, t % SLOTS
                wait(pe, s_prod, tile, UNITS, 2 * t + 2)
                if slot == 0:
                    wait(pe, s_z, tile, ZBANKS, bank - 1)
                for q in range(STEP):
                    last = pe.matmul(z_ps[bank % 2][32 * q:32 * q + 32, :], lhsT=sel[:, slot, :],
                                     rhs=prod[:, (2 * t + q // 2) % PROD_RING, q % 2, :],
                                     start=(slot == 0), stop=(slot == SLOTS - 1 or t == STEPS - 1))
                last.then_inc(s_red, 1)

            def tower(tile, n):
                wait(pe, s_act, tile, MLP, n + 1 - MLP)
                if n == 0:
                    pe.wait_ge(s_par, 80)
                    wait(pe, s_z, tile, ZBANKS, -1)
                if n < H1 // P:
                    for G in range(ZBANKS):
                        if n == 0 and G == ZBANKS - 1:
                            wait(pe, s_dense, tile, 64, 0)
                        last = pe.matmul(mlp_ps[:, :], lhsT=w1_sb[:, G, n * P:(n + 1) * P], rhs=z_sb[:, G, :],
                                         start=(G == 0), stop=(G == ZBANKS - 1))
                elif n < MLP - 1:
                    c = n - H1 // P
                    for G in range(H1 // P):
                        last = pe.matmul(mlp_ps[:, :], lhsT=w2_sb[:, G, c * P:(c + 1) * P], rhs=h1_sb[:, G, :],
                                         start=(G == 0), stop=(G == H1 // P - 1))
                else:
                    for G in range(H2 // P):
                        last = pe.matmul(mlp_ps[0:1, :], lhsT=w3_sb[:, G:G + 1], rhs=h2_sb[:, G, :],
                                         start=(G == 0), stop=(G == H2 // P - 1))
                last.then_inc(s_tower, 1)

            def body(tile):
                first = isinstance(tile, int)
                for ev in SCHEDULE:
                    if ev[0] == "T":
                        turn(tile, ev[1])
                    elif ev[0] == "M" and not first:
                        tower(tile, ev[1])
                    elif ev[0] == "S":
                        project(tile, 2 * ev[1])
                        project(tile, 2 * ev[1] + 1)
                        if ev[1]:
                            reduce(tile, ev[1] - 1)
                    elif ev[0] == "R":
                        reduce(tile, STEPS - 1)

            over_tiles(pe, body)
            for n in range(MLP):
                tower(TILES, n)


def kernel(**inputs):
    import concourse.bacc as bacc
    from concourse.bass_utils import run_bass_kernel_spmd

    a = {k: np.asarray(v) for k, v in inputs.items()}
    twin_rows = np.array([[pair_row(*p) for p in chunk_pairs(c)] for c in TWIN_CHUNKS])
    odd_rows = np.array([[pair_row(*p) for p in chunk_pairs(CHUNKS[CHUNK_OF_ODD[g]])] for g in range(ODD)])
    z_rows = np.zeros(ZBANKS * P, np.int64)
    for c, chunk in enumerate(CHUNKS):
        for half, p in enumerate(chunk_pairs(chunk)):
            z_rows[z_row(c, half)] = pair_row(*p)
    for d in range(DENSE):
        z_rows[dense_row(d)] = FIELDS * (FIELDS - 1) // 2 + d

    w = a["L0_rec_w"]
    arrays = {
        "ids": a["ids"].reshape(TILES, BLOCKS, P, FIELDS).transpose(0, 2, 1, 3).reshape(TILES, P, BLOCKS * FIELDS),
        "dense": a["dense_ctx"].reshape(TILES, TB, DENSE).transpose(0, 2, 1),
        "w_twin": w[twin_rows].reshape(WGROUPS, WG, 2, EMBED, EMBED).transpose(0, 3, 1, 2, 4)
                  .reshape(WGROUPS, EMBED, WCOLS),
        "w_odd": w[odd_rows].transpose(2, 0, 1, 3),
        "w1": a["W_top1"][z_rows].reshape(ZBANKS, P, H1).transpose(1, 0, 2),
        "b1": a["b_top1"].reshape(H1 // P, P).T,
        "w2": a["W_top2"].reshape(H1 // P, P, H2).transpose(1, 0, 2),
        "b2": a["b_top2"].reshape(H2 // P, P).T,
        "w3": a["W_top3"].reshape(H2 // P, P).T,
    }
    arrays |= {f"tbl_{f}": a[f"tbl_{f}"] for f in range(FIELDS)}
    arrays = {k: np.ascontiguousarray(v) for k, v in arrays.items()}

    nc = bacc.Bacc("TRN2", target_bir_lowering=False, num_devices=1)
    ap = {k: nc.dram_tensor(k, v.shape, mybir.dt.from_np(v.dtype), kind="ExternalInput").ap()
          for k, v in arrays.items()}
    out = nc.dram_tensor("out", (TILES, 1, TB), mybir.dt.float32, kind="ExternalOutput").ap()
    tower_kernel(nc, ap["ids"], [ap[f"tbl_{f}"] for f in range(FIELDS)], ap["dense"], ap["w_twin"], ap["w_odd"],
                 ap["w1"], ap["b1"], ap["w2"], ap["b2"], ap["w3"], out)
    r = run_bass_kernel_spmd(nc, [arrays], core_ids=[0])
    return r.results[0]["out"].reshape(BATCH, 1)
```

```python
from contextlib import ExitStack

import concourse.bass as bass
import numpy as np
from concourse import mybir

FIELDS, EMBED, BATCH, DENSE = 32, 64, 2048, 16
H1, H2 = 512, 256
P = 128
TB = 512
TILES = BATCH // TB
BLOCKS = TB // P
TWINS = FIELDS // 2


def pair_row(i, j):
    return i * (2 * FIELDS - i - 1) // 2 + j - i - 1


def chunk_order():
    chunks = []
    for i in range(FIELDS - 2, -1, -1):
        chunks += [("twin", i, m) for m in range(i // 2 + 1, TWINS)]
        if i % 4 == 0:
            chunks.append(("odd", i, i // 4))
    return chunks


CHUNKS = chunk_order()
STEP = 4
STEPS = len(CHUNKS) // STEP
UNITS = len(CHUNKS) // 2
SLOTS = 32 // 2
ZBANKS = 4
TWIN_CHUNKS = [c for c in CHUNKS if c[0] == "twin"]
ODD = FIELDS // 4
LAG = 2
WG = 8
WGROUPS = len(TWIN_CHUNKS) // WG
SPLITS = WGROUPS // 2
WCOLS = WG * P
MLP = H1 // P + H2 // P + 1


def chunk_pairs(chunk):
    kind, i, m = chunk
    if kind == "twin":
        return [(i, 2 * m), (i, 2 * m + 1)]
    return [(4 * m, 4 * m + 1), (4 * m + 2, 4 * m + 3)]


def z_row(c, half):
    bank, step, group = c // (STEP * SLOTS), c % (STEP * SLOTS) // STEP, c % STEP
    return bank * P + 32 * group + 2 * step + half


def dense_row(d):
    return (ZBANKS - 1) * P + 32 * (d // 4) + 28 + d % 4


GATHER_RING, MOV_RING, W_RING, RAW_RING, PROJ_RING, PROD_RING = 8, 6, 8, 2, 3, 8
KEEP_FROM = 1
W_AHEAD = 3


def tile_schedule(first):
    group_end = {}
    seen = 0
    for c, chunk in enumerate(CHUNKS):
        if chunk[0] == "twin":
            seen += 1
            if seen % WG == 0:
                group_end[seen // WG - 1] = c // STEP

    def first_step(k):
        return min(c for c, (_, i, _) in enumerate(CHUNKS) if i <= FIELDS - 1 - 2 * k) // STEP

    def arrives(k):
        return 2.9 * (k + 1) + 2.7

    if first:
        ev = [("P", 0), ("T", 0), ("P", 1), ("Q", 0), ("T", 1), ("K", 0), ("Q", 1), ("K", 1), ("P", 2), ("T", 2),
              ("Q", 2), ("K", 2)]
        keep = [3, 4, 5]
    else:
        ev = [("W", 0), ("W", 1), ("W", 2), ("T", 0), ("R", STEPS - 2), ("R", STEPS - 1),
              ("Z", ZBANKS - 1), ("T", 1), ("M", 0), ("T", 2), ("M", 1), ("T", 3)]
    next_t, next_m, next_w, next_p, begun, clock = 3 if first else 4, 2, W_AHEAD, 3, None, arrives(2) + 1.5
    for t in range(STEPS):
        lowest = min(i for _, i, _ in CHUNKS[STEP * t:STEP * t + STEP])
        needed = (FIELDS - 1 - lowest) // 2
        while next_t < TWINS and (first and (next_t <= needed or clock >= arrives(next_t) and next_t <= needed + 1)
                                  or not first and t >= max(first_step(next_t) - 3, next_t - 2)):
            if next_t == needed:
                clock = max(clock, arrives(next_t) + 2.2)
            ev.append(("T", next_t))
            next_t += 1
        ev.append(("A", t))
        if t >= SLOTS and (t - LAG) % SLOTS == SLOTS - 1:
            ev.append(("Z", t // SLOTS - 1))
        if next_m < MLP:
            ev.append(("M", next_m))
            next_m += 1
        ev.append(("B", t))
        clock += 1
        if not first:
            while next_w < WGROUPS and group_end[next_w - W_AHEAD] <= t:
                ev.append(("W", next_w))
                next_w += 1
        elif begun is not None:
            ev.append(("Q", begun))
            keep += [2 * begun, 2 * begun + 1]
            begun = None
        elif next_p < SPLITS and (2 * next_p < W_RING or group_end[2 * next_p + 1 - W_RING] <= t - 1
                                    and 2 * next_p + 1 - W_RING not in keep):
            ev.append(("P", next_p))
            next_p, begun = next_p + 1, next_p
        if first and keep and t >= KEEP_FROM:
            ev.append(("K", keep.pop(0)))
        if t == MLP:
            ev.append(("D",))
    return ev


CHUNK_OF_ODD = {m: c for c, (kind, _, m) in enumerate(CHUNKS) if kind == "odd"}
TWIN_INDEX = {c: n for n, c in enumerate(c for c, x in enumerate(CHUNKS) if x[0] == "twin")}


def last_unit_of_source(i):
    mine = [c for c, (kind, a, m) in enumerate(CHUNKS) if a == i or (kind == "odd" and i == 4 * m + 2)]
    return max(mine) // 2


def last_unit_of_group(g):
    return max(c for c, n in TWIN_INDEX.items() if n // WG == g) // 2


def mov_slot(i):
    return (FIELDS - 2 - i) % MOV_RING


def mov_uses(i):
    slot = mov_slot(i)
    per = len(range(slot, FIELDS - 1, MOV_RING))
    return per, (FIELDS - 2 - i) // MOV_RING + 1


def w_uses(g):
    return len(range(g % W_RING, WGROUPS, W_RING)), g // W_RING + 1


def tower_kernel(nc, ids, tables, dense, w_twin, w_odd, w1, b1, w2, b2, w3, out):
    fp32, f32r, i32 = mybir.dt.float32, mybir.dt.float32r, mybir.dt.int32
    ALU, ACT = mybir.AluOpType, mybir.ActivationFunctionType

    w_split = nc.dram_tensor("w_split", (WGROUPS, P, WCOLS), fp32, kind="Internal").ap()

    with ExitStack() as ctx:
        def sb(name, shape, dt=fp32):
            return ctx.enter_context(nc.sbuf_tensor(name, shape, dt))

        def ps(name, shape):
            return ctx.enter_context(nc.psum_tensor(name, shape, fp32))

        def sem(name):
            return ctx.enter_context(nc.semaphore(name))

        ids_sb = sb("ids_sb", [P, BLOCKS * FIELDS], i32)
        rows = sb("rows", [P, GATHER_RING, BLOCKS, P])
        vT = sb("vT", [P, TWINS, TB])
        v_odd = sb("v_odd", [P, 2, TB])
        halves = sb("halves", [P, 2, 2, TB], f32r)
        mov = sb("mov", [P, MOV_RING, 2, TB], f32r)
        w_raw = sb("w_raw", [P, RAW_RING, WCOLS])
        w_ring = sb("w_ring", [P, W_RING, WCOLS], f32r)
        w_odd_raw = sb("w_odd_raw", [P, ODD, 2, EMBED])
        w_odd_sb = sb("w_odd_sb", [P, ODD, 3, EMBED], f32r)
        prod = sb("prod", [P, PROD_RING, 2, TB])
        sel = sb("sel", [P, SLOTS, 32])
        ident = sb("ident", [P, P])
        z_sb = sb("z_sb", [P, ZBANKS, TB])
        h1_sb = sb("h1_sb", [P, H1 // P, TB])
        h2_sb = sb("h2_sb", [P, H2 // P, TB])
        y_sb = sb("y_sb", [P, TB // 4])
        w1_sb = sb("w1_sb", [P, ZBANKS, H1])
        w2_sb = sb("w2_sb", [P, H1 // P, H2])
        w3_sb = sb("w3_sb", [P, H2 // P])
        b1_sb = sb("b1_sb", [P, H1 // P])
        b2_sb = sb("b2_sb", [P, H2 // P])

        proj = [ps(f"proj{n}", [P, 2, TB]) for n in range(PROJ_RING)]
        z_ps = ps("z_ps", [P, TB])
        desk_ps = ps("desk_ps", [P, TB])

        desks = [proj[PROJ_RING - 1][:, 0, :], proj[PROJ_RING - 1][:, 1, :]] + (MLP - 2) * [desk_ps[:, :]]
        tail_desks = [(desk_ps[:, :], proj[0][:, 0, :])[n % 2] for n in range(MLP)]

        s_passed = sem("waits_passed")
        s_ids = sem("ids_loaded")
        s_rows = [sem(f"rows_gathered{n}") for n in range(GATHER_RING)]
        s_ident = sem("ident_made")
        s_sel = sem("sel_made")
        s_par = sem("parameters_loaded")
        s_oraw = sem("w_odd_loaded")
        s_ohi = sem("w_odd_hi")
        s_olo = sem("w_odd_split")
        s_raw = [sem(f"w_raw_loaded{n}") for n in range(RAW_RING)]
        s_whi = sem("w_hi")
        s_wlo = sem("w_lo")
        s_lomoved = sem("w_lo_moved")
        s_wsp = sem("w_split_done")
        s_scr = [sem(f"w_stored{n}") for n in range(W_RING)]
        s_w = [sem(f"w_loaded{n}") for n in range(W_RING)]
        s_turn = sem("turned")
        s_vt = sem("vt_written")
        s_hi = sem("e_hi")
        s_lo = sem("e_lo")
        s_mov = [sem(f"mov_loaded{n}") for n in range(MOV_RING)]
        s_vodd = [sem(f"v_odd_loaded{n}") for n in range(2)]
        s_proj = sem("projected")
        s_prod = sem("multiplied")
        s_red = sem("reduced")
        s_z = sem("z_copied")
        s_dense = sem("dense_loaded")
        s_tower = sem("tower_summed")
        s_act = sem("tower_activated")
        s_out = sem("out_stored")

        block = ctx.enter_context(nc.Block())

        def wait(eng, s, tile, per_tile, count):
            value = tile * per_tile + count
            if not isinstance(tile, int) or value > 0:
                eng.wait_ge(s, value)
            if not isinstance(tile, int) and eng in alone:
                eng.sem_inc(s_passed, 1)

        alone = []

        def over_tiles(eng, body):
            body(0)
            with eng.Fori(1, TILES) as tile:
                body(tile)

        @block.gpsimd
        def _(pool):
            alone.append(pool)
            def make_identity():
                pool.memset(ident[:, :], 0.0).then_inc(s_ident, 1)
                pool.wait_ge(s_ident, 1)
                pool.affine_select(out=ident[:, :], in_=ident[:, :], compare_op=ALU.not_equal, fill=1.0,
                                   base=0, pattern=[[-1, P]], channel_multiplier=1).then_inc(s_ident, 1)

            def body(tile):
                for n in range(GATHER_RING):
                    wait(pool, s_rows[n], tile, 2 * 128, 0)
                pool.dma_start(ids_sb[:, :], ids[tile, :, :]).then_inc(s_ids, 16)
                if isinstance(tile, int):
                    make_identity()
                wait(pool, s_ids, tile, 16, 16)
                for k in range(TWINS):
                    wait(pool, s_turn, tile, TWINS, k - GATHER_RING + 1)
                    for blk in range(BLOCKS):
                        for half in range(2):
                            field = 2 * (TWINS - 1 - k) + half
                            at = blk * FIELDS + field
                            pool.indirect_dma_start(
                                rows[:, k % GATHER_RING, blk, half * EMBED:(half + 1) * EMBED], None,
                                tables[field],
                                bass.IndirectOffsetOnAxis(ap=ids_sb[:, at:at + 1], axis=0),
                            ).then_inc(s_rows[k % GATHER_RING], 16)

            over_tiles(pool, body)

        @block.sync
        def _(sp):
            alone.append(sp)
            def load_raw(j):
                if j >= RAW_RING:
                    sp.wait_ge(s_wsp, j - RAW_RING + 1)
                sp.dma_start(w_raw[:, j % RAW_RING, :], w_twin[2 * j:2 * j + 2, :, :]
                             .rearrange("g k c -> (g k) c")).then_inc(s_raw[j % RAW_RING], 16)

            def store_split(g):
                sp.wait_ge(s_wsp, g // 2 + 1)
                sp.dma_start(w_split[g, :, :], w_ring[:, g % W_RING, :].bitcast(fp32)).then_inc(s_scr[g % W_RING], 16)

            def weights(tile, g):
                before = g - W_RING if g >= W_RING else max(range(g % W_RING, WGROUPS, W_RING))
                wait(sp, s_proj, tile, UNITS, last_unit_of_group(before) + 1 - (UNITS if g < W_RING else 0))
                sp.wait_ge(s_scr[g % W_RING], 16 * w_uses(g)[1])
                sp.dma_start(w_ring[:, g % W_RING, :].bitcast(fp32), w_split[g, :, :]).then_inc(s_w[g % W_RING], 16)

            def sources(tile, k):
                m = TWINS - 1 - k
                wait(sp, s_lo, tile, TWINS, k + 1)
                for i in (2 * m + 1, 2 * m):
                    if i == FIELDS - 1:
                        continue
                    before = i + MOV_RING
                    if before <= FIELDS - 2:
                        wait(sp, s_proj, tile, UNITS, last_unit_of_source(before) + 1)
                    else:
                        before = min(x for x in range(FIELDS - 1) if mov_slot(x) == mov_slot(i))
                        wait(sp, s_proj, tile, UNITS, last_unit_of_source(before) + 1 - UNITS)
                    src = halves[(i % 2) * EMBED:(i % 2 + 1) * EMBED, k % 2, :, :].bitcast(fp32)
                    for half in range(2):
                        sp.dma_start(mov[half * EMBED:(half + 1) * EMBED, mov_slot(i), :, :].bitcast(fp32),
                                     src).then_inc(s_mov[mov_slot(i)], 16)
                if m % 2 == 0:
                    g = m // 2
                    wait(sp, s_vt, tile, TWINS, k + 1)
                    if g + 2 < ODD:
                        wait(sp, s_prod, tile, UNITS, CHUNK_OF_ODD[g + 2] // 2 + 1)
                    else:
                        wait(sp, s_prod, tile, UNITS, CHUNK_OF_ODD[g % 2] // 2 + 1 - UNITS)
                    for half in range(2):
                        sp.dma_start(v_odd[half * EMBED:(half + 1) * EMBED, g % 2, :],
                                     vT[EMBED:P, m + half, :]).then_inc(s_vodd[g % 2], 16)

            def dense_rows(tile):
                wait(sp, s_tower, tile, MLP, H1 // P - MLP)
                for q in range(4):
                    sp.dma_start(z_sb[32 * q + 28:32 * q + 32, ZBANKS - 1, :],
                                 dense[tile, 4 * q:4 * q + 4, :]).then_inc(s_dense, 16)

            def result(tile):
                wait(sp, s_act, tile, MLP, 1)
                sp.dma_start(out[tile - 1, :, :], y_sb[0:P:32, :]).then_inc(s_out, 16)

            def body(tile):
                first = isinstance(tile, int)
                for ev in tile_schedule(first):
                    if ev[0] == "W" and not first:
                        weights(tile, ev[1])
                    elif ev[0] == "P":
                        for j in (range(RAW_RING) if ev[1] == 0 else ()):
                            load_raw(j)
                    elif ev[0] == "K":
                        store_split(ev[1])
                    elif ev[0] == "Q" and ev[1] + RAW_RING < SPLITS:
                        load_raw(ev[1] + RAW_RING)
                    elif ev[0] == "T":
                        sources(tile, ev[1])
                    elif ev[0] == "D":
                        dense_rows(tile)
                    elif ev == ("M", MLP - 1) and not first:
                        result(tile)

            over_tiles(sp, body)
            result(TILES)
            sp.wait_ge(s_out, 16 * TILES + 16)

        @block.scalar
        def _(act):
            for half in range(2):
                act.dma_start(w_odd_raw[half * EMBED:(half + 1) * EMBED, :, :, :], w_odd).then_inc(s_oraw, 16)
            act.sem_inc(s_act, 1)
            act.sem_inc(s_out, 16)
            act.wait_ge(s_oraw, 32)
            act.wait_ge(s_ohi, 1)
            act.activation(w_odd_sb[:, :, 0:3:2, :], w_odd_raw[:, :, :, :], ACT.Copy).then_inc(s_ohi, 1)

            def load_parameters():
                act.dma_start(w1_sb[:, :, :], w1).then_inc(s_par, 16)
                act.dma_start(w2_sb[:, :, :], w2).then_inc(s_par, 16)
                act.dma_start(w3_sb[:, :], w3).then_inc(s_par, 16)
                act.dma_start(b1_sb[:, :], b1).then_inc(s_par, 16)
                act.dma_start(b2_sb[:, :], b2).then_inc(s_par, 16)

            def weights_hi(j):
                even, odd = 2 * j, 2 * j + 1
                act.wait_ge(s_raw[j % RAW_RING], 16 * (j // RAW_RING + 1))
                if even >= W_RING:
                    act.wait_ge(s_proj, last_unit_of_group(odd - W_RING) + 1)
                    for g in (even, odd):
                        act.wait_ge(s_scr[g % W_RING], 16 * (g // W_RING))
                act.activation(w_ring[:, even % W_RING, :], w_raw[:, j % RAW_RING, :], ACT.Copy).then_inc(s_whi, 1)

            def weights_placed(j):
                even, odd = 2 * j % W_RING, (2 * j + 1) % W_RING
                act.wait_ge(s_wlo, j + 1)
                act.activation(w_ring[EMBED:P, even, :], w_ring[0:EMBED, odd, :].bitcast(fp32),
                               ACT.Copy).then_inc(s_lomoved, 1)
                act.wait_ge(s_lomoved, j + 1)
                act.activation(w_ring[0:EMBED, odd, :], w_raw[EMBED:P, j % RAW_RING, :], ACT.Copy).then_inc(s_wsp, 1)

            def turned(tile, k):
                m = TWINS - 1 - k
                wait(act, s_turn, tile, TWINS, k + 1)
                if k == 0:
                    wait(act, s_prod, tile, UNITS, 0)
                act.activation(vT[:, m, :], desk_ps[:, :], ACT.Copy).then_inc(s_vt, 1)
                before = m + 2 if k >= 2 else 1 - k
                for i in (2 * before, 2 * before + 1):
                    if i < FIELDS - 1:
                        per, use = mov_uses(i)
                        wait(act, s_mov[mov_slot(i)], tile, 32 * per, 32 * (use if k >= 2 else use - per))
                act.activation(halves[:, k % 2, 0, :], desk_ps[:, :], ACT.Copy).then_inc(s_hi, 1)

            def tower(tile, n, banks):
                mlp_ps = banks[n]
                wait(act, s_tower, tile, MLP, n + 1 - MLP)
                if n < H1 // P:
                    act.activation(h1_sb[:, n, :], mlp_ps, ACT.Relu,
                                   bias=b1_sb[:, n:n + 1]).then_inc(s_act, 1)
                elif n < MLP - 1:
                    c = n - H1 // P
                    act.activation(h2_sb[:, c, :], mlp_ps, ACT.Relu,
                                   bias=b2_sb[:, c:c + 1]).then_inc(s_act, 1)
                else:
                    wait(act, s_out, tile, 16, 0)
                    act.activation(y_sb[:, :], mlp_ps[:, 0:TB // 4], ACT.Copy).then_inc(s_act, 1)

            def z_copy(tile, G):
                wait(act, s_red, tile, STEPS, SLOTS * (G + 1) if G < ZBANKS - 1 else 0)
                if G < ZBANKS - 1:
                    act.activation(z_sb[:, G, :], z_ps[:, :], ACT.Copy).then_inc(s_z, 1)
                    return
                for q in range(4):
                    part = slice(32 * q, 32 * q + 28)
                    last = act.activation(z_sb[part, G, :], z_ps[part, :], ACT.Copy)
                last.then_inc(s_z, 1)

            def body(tile):
                first = isinstance(tile, int)
                for ev in tile_schedule(first):
                    if ev[0] == "P":
                        weights_hi(ev[1])
                    elif ev[0] == "Q":
                        weights_placed(ev[1])
                    elif ev[0] == "T":
                        turned(tile, ev[1])
                        if first and ev[1] == TWINS - 1:
                            load_parameters()
                    elif ev[0] == "M" and not first:
                        tower(tile, ev[1], desks)
                    elif ev[0] == "Z" and not (first and ev[1] == ZBANKS - 1):
                        z_copy(tile, ev[1])
                if first:
                    act.wait_ge(s_par, 80)

            over_tiles(act, body)
            z_copy(TILES, ZBANKS - 1)
            for n in range(MLP):
                tower(TILES, n, tail_desks)

        @block.vector
        def _(dve):
            dve.memset(w_odd_sb[:, :, :, :].bitcast(fp32), 0.0).then_inc(s_ohi, 1)
            dve.memset(sel[:, :, :], 0.0).then_inc(s_sel, 1)
            dve.wait_ge(s_sel, 1)
            flat = sel[:, :, :].rearrange("p s c -> p (s c)")
            for half in range(2):
                last = 34 * (SLOTS - 1) + half
                dve.memset(flat[half * EMBED:(half + 1) * EMBED, half:last + 1:34], 1.0).then_inc(s_sel, 1)
            dve.wait_ge(s_ohi, 2)
            dve.tensor_tensor(w_odd_sb[EMBED:P, :, 0:3:2, :], w_odd_raw[EMBED:P, :, :, :],
                              w_odd_sb[EMBED:P, :, 0:3:2, :].bitcast(fp32), ALU.subtract).then_inc(s_olo, 1)

            def weights_lo(j):
                dve.wait_ge(s_whi, j + 1)
                dve.tensor_tensor(w_ring[:, (2 * j + 1) % W_RING, :], w_raw[:, j % RAW_RING, :],
                                  w_ring[:, 2 * j % W_RING, :].bitcast(fp32), ALU.subtract).then_inc(s_wlo, 1)

            def lo(tile, k):
                wait(dve, s_vt, tile, TWINS, k + 1)
                wait(dve, s_hi, tile, TWINS, k + 1)
                dve.tensor_tensor(halves[:, k % 2, 1, :], vT[:, TWINS - 1 - k, :],
                                  halves[:, k % 2, 0, :].bitcast(fp32), ALU.subtract).then_inc(s_lo, 1)

            def multiply(tile, u):
                a, b = CHUNKS[2 * u], CHUNKS[2 * u + 1]
                wait(dve, s_proj, tile, UNITS, u + 1)
                before = u - PROD_RING if u >= PROD_RING else max(range(u, UNITS, PROD_RING)) - UNITS
                wait(dve, s_red, tile, STEPS, before // 2 + 1)
                if a[0] == b[0] == "twin" and a[2] < b[2]:
                    dve.tensor_tensor(prod[:, u % PROD_RING, :, :], proj[u % PROJ_RING][:, :, :],
                                      vT[:, a[2]:b[2] + 1:b[2] - a[2], :], ALU.mult).then_inc(s_prod, 1)
                    return
                for n, (kind, _, m) in enumerate((a, b)):
                    if kind == "odd":
                        wait(dve, s_vodd[m % 2], tile, 32 * ODD // 2, 32 * ((ODD - 1 - m) // 2 + 1))
                    target = vT[:, m, :] if kind == "twin" else v_odd[:, m % 2, :]
                    last = dve.tensor_tensor(prod[:, u % PROD_RING, n, :], proj[u % PROJ_RING][:, n, :], target, ALU.mult)
                last.then_inc(s_prod, 1)

            def body(tile):
                first = isinstance(tile, int)
                for ev in tile_schedule(first):
                    if ev[0] == "P":
                        weights_lo(ev[1])
                    elif ev[0] == "T":
                        lo(tile, ev[1])
                    elif ev[0] in "AB":
                        multiply(tile, 2 * ev[1] + (ev[0] == "B"))

            over_tiles(dve, body)

        @block.tensor
        def _(pe):
            pe.wait_ge(s_ident, 2)
            pe.wait_ge(s_sel, 3)
            pe.wait_ge(s_olo, 1)

            def turn(tile, k):
                wait(pe, s_rows[k % GATHER_RING], tile, 2 * 128, 128 * (k // GATHER_RING + 1))
                wait(pe, s_hi, tile, TWINS, k)
                for blk in range(BLOCKS):
                    last = pe.transpose(desk_ps[:, blk * P:(blk + 1) * P],
                                        rows[:, k % GATHER_RING, blk, :], ident[:, :])
                last.then_inc(s_turn, 1)

            def weights_ready(tile, g):
                if isinstance(tile, int):
                    pe.wait_ge(s_wsp, g // 2 + 1)
                else:
                    per, use = w_uses(g)
                    wait(pe, s_w[g % W_RING], tile, 16 * per, 16 * (use - per))

            def source_ready(tile, i):
                per, use = mov_uses(i)
                wait(pe, s_mov[mov_slot(i)], tile, 32 * per, 32 * use)

            def project(tile, u):
                before = u - PROJ_RING if u >= PROJ_RING else max(range(u, UNITS, PROJ_RING)) - UNITS
                wait(pe, s_prod, tile, UNITS, before + 1)
                if u == PROJ_RING - 1 and not isinstance(tile, int):
                    wait(pe, s_act, tile, MLP, 3 - MLP)
                for n in range(2):
                    c = 2 * u + n
                    kind, i, m = CHUNKS[c]
                    if kind == "twin":
                        w = TWIN_INDEX[c]
                        if w % WG == 0:
                            weights_ready(tile, w // WG)
                        if m == i // 2 + 1:
                            source_ready(tile, i)
                        wt = w_ring[:, (w // WG) % W_RING, (w % WG) * P:(w % WG + 1) * P]
                        parts = [(wt, i)]
                    else:
                        if m == ODD - 1:
                            source_ready(tile, i + 2)
                        wo = w_odd_sb[:, m, :, :].rearrange("p a l -> p (a l)")
                        parts = [(wo[:, 0:P], i), (wo[:, EMBED:EMBED + P], i + 2)]
                    passes = [(wt, src, part) for wt, src in parts for part in range(2)]
                    for x, (wt, src, part) in enumerate(passes):
                        last = pe.matmul(proj[u % PROJ_RING][:, n, :], lhsT=wt, rhs=mov[:, mov_slot(src), part, :],
                                         start=(x == 0), stop=(x == len(passes) - 1))
                last.then_inc(s_proj, 1)

            def reduce(tile, t, ago=0):
                bank, slot = t // SLOTS, t % SLOTS
                wait(pe, s_prod, tile, UNITS, 2 * t + 2 - ago * UNITS)
                if slot == 0:
                    wait(pe, s_z, tile, ZBANKS, bank)
                for q in range(STEP):
                    last = pe.matmul(z_ps[32 * q:32 * q + 32, :], lhsT=sel[:, slot, :],
                                     rhs=prod[:, (2 * t + q // 2) % PROD_RING, q % 2, :],
                                     start=(slot == 0), stop=(slot == SLOTS - 1 or t == STEPS - 1))
                last.then_inc(s_red, 1)

            def tower(tile, n, banks):
                mlp_ps = banks[n]
                tail = banks is tail_desks
                if tail:
                    wait(pe, s_act, tile, MLP, n + (n == MLP - 1) - MLP)
                elif n == 0 or n >= 3:
                    wait(pe, s_act, tile, MLP, n + 1 - MLP)
                if n == 0:
                    pe.wait_ge(s_par, 80)
                    wait(pe, s_z, tile, ZBANKS, -1)
                if n < H1 // P:
                    for G in range(ZBANKS):
                        if n == 0 and G == ZBANKS - 1:
                            wait(pe, s_z, tile, ZBANKS, 0)
                            wait(pe, s_dense, tile, 64, 0)
                        last = pe.matmul(mlp_ps, lhsT=w1_sb[:, G, n * P:(n + 1) * P], rhs=z_sb[:, G, :],
                                         start=(G == 0), stop=(G == ZBANKS - 1))
                elif n < MLP - 1:
                    c = n - H1 // P
                    for G in range(H1 // P):
                        if tail and c == 0:
                            wait(pe, s_act, tile, MLP, G + 2 - MLP)
                        last = pe.matmul(mlp_ps, lhsT=w2_sb[:, G, c * P:(c + 1) * P], rhs=h1_sb[:, G, :],
                                         start=(G == 0), stop=(G == H1 // P - 1))
                else:
                    for G in range(H2 // P):
                        for q in range(4):
                            last = pe.matmul(mlp_ps[32 * q:32 * q + 1, 0:TB // 4], lhsT=w3_sb[:, G:G + 1],
                                             rhs=h2_sb[:, G, q * TB // 4:(q + 1) * TB // 4],
                                             start=(G == 0), stop=(G == H2 // P - 1))
                last.then_inc(s_tower, 1)

            def body(tile):
                first = isinstance(tile, int)
                turns = items = 0
                for ev in tile_schedule(first):
                    if ev[0] == "T":
                        if items > 2 and not first:
                            wait(pe, s_act, tile, MLP, items + 1 - MLP)
                        turn(tile, ev[1])
                        turns += 1
                    elif ev[0] == "M" and not first:
                        if items >= 2:
                            wait(pe, s_hi, tile, TWINS, turns)
                        tower(tile, ev[1], desks)
                        items += 1
                    elif ev[0] == "A":
                        project(tile, 2 * ev[1])
                        if ev[1] > LAG and (ev[1] - LAG) % 2:
                            reduce(tile, ev[1] - LAG - 1)
                            reduce(tile, ev[1] - LAG)
                    elif ev[0] == "B":
                        project(tile, 2 * ev[1] + 1)
                    elif ev[0] == "R" and not first:
                        reduce(tile, ev[1], ago=1)

            over_tiles(pe, body)
            for t in range(STEPS - LAG, STEPS):
                reduce(TILES, t, ago=1)
            for n in range(MLP):
                tower(TILES, n, tail_desks)


def kernel(**inputs):
    import concourse.bacc as bacc
    from concourse.bass_utils import run_bass_kernel_spmd

    a = {k: np.asarray(v) for k, v in inputs.items()}
    twin_rows = np.array([[pair_row(*p) for p in chunk_pairs(c)] for c in TWIN_CHUNKS])
    odd_rows = np.array([[pair_row(*p) for p in chunk_pairs(CHUNKS[CHUNK_OF_ODD[g]])] for g in range(ODD)])
    z_rows = np.zeros(ZBANKS * P, np.int64)
    for c, chunk in enumerate(CHUNKS):
        for half, p in enumerate(chunk_pairs(chunk)):
            z_rows[z_row(c, half)] = pair_row(*p)
    for d in range(DENSE):
        z_rows[dense_row(d)] = FIELDS * (FIELDS - 1) // 2 + d

    w = a["L0_rec_w"]
    arrays = {
        "ids": a["ids"].reshape(TILES, BLOCKS, P, FIELDS).transpose(0, 2, 1, 3).reshape(TILES, P, BLOCKS * FIELDS),
        "dense": a["dense_ctx"].reshape(TILES, TB, DENSE).transpose(0, 2, 1),
        "w_twin": w[twin_rows].reshape(WGROUPS, WG, 2, EMBED, EMBED).transpose(0, 3, 1, 2, 4)
                  .reshape(WGROUPS, EMBED, WCOLS),
        "w_odd": w[odd_rows].transpose(2, 0, 1, 3),
        "w1": a["W_top1"][z_rows].reshape(ZBANKS, P, H1).transpose(1, 0, 2),
        "b1": a["b_top1"].reshape(H1 // P, P).T,
        "w2": a["W_top2"].reshape(H1 // P, P, H2).transpose(1, 0, 2),
        "b2": a["b_top2"].reshape(H2 // P, P).T,
        "w3": a["W_top3"].reshape(H2 // P, P).T,
    }
    arrays |= {f"tbl_{f}": a[f"tbl_{f}"] for f in range(FIELDS)}
    arrays = {k: np.ascontiguousarray(v) for k, v in arrays.items()}

    nc = bacc.Bacc("TRN2", target_bir_lowering=False, num_devices=1)
    ap = {k: nc.dram_tensor(k, v.shape, mybir.dt.from_np(v.dtype), kind="ExternalInput").ap()
          for k, v in arrays.items()}
    out = nc.dram_tensor("out", (TILES, 4, TB // 4), mybir.dt.float32, kind="ExternalOutput").ap()
    tower_kernel(nc, ap["ids"], [ap[f"tbl_{f}"] for f in range(FIELDS)], ap["dense"], ap["w_twin"], ap["w_odd"],
                 ap["w1"], ap["b1"], ap["w2"], ap["b2"], ap["w3"], out)
    r = run_bass_kernel_spmd(nc, [arrays], core_ids=[0])
    return r.results[0]["out"].reshape(BATCH, 1)
```

```python
from contextlib import ExitStack

import concourse.bass as bass
import numpy as np
from concourse import mybir

FIELDS, EMBED, BATCH, DENSE = 32, 64, 2048, 16
H1, H2 = 512, 256
P = 128
TB = 512
TILES = BATCH // TB
BLOCKS = TB // P
TWINS = FIELDS // 2
SOURCES = FIELDS - 1


def pair_row(i, j):
    return i * (2 * FIELDS - i - 1) // 2 + j - i - 1


def chunk_order():
    chunks = []
    for i in range(FIELDS - 2, -1, -1):
        chunks += [("twin", i, m) for m in range(i // 2 + 1, TWINS)]
        if i % 4 == 0:
            chunks.append(("odd", i, i // 4))
    return chunks


CHUNKS = chunk_order()
STEP = 4
STEPS = len(CHUNKS) // STEP
UNITS = len(CHUNKS) // 2
SLOTS = 32 // 2
ZBANKS = 4
TWIN_CHUNKS = [c for c in CHUNKS if c[0] == "twin"]
ODD = FIELDS // 4
LAG = 2
WG = 8
WGROUPS = len(TWIN_CHUNKS) // WG
SPLITS = WGROUPS // 2
WCOLS = WG * P
MLP = H1 // P + H2 // P + 1


def chunk_pairs(chunk):
    kind, i, m = chunk
    if kind == "twin":
        return [(i, 2 * m), (i, 2 * m + 1)]
    return [(4 * m, 4 * m + 1), (4 * m + 2, 4 * m + 3)]


def z_row(c, half):
    bank, step, group = c // (STEP * SLOTS), c % (STEP * SLOTS) // STEP, c % STEP
    return bank * P + 32 * group + 2 * step + half


def dense_row(d):
    return (ZBANKS - 1) * P + 32 * (d // 4) + 28 + d % 4


GATHER_RING, MOV_RING, W_RING, RAW_RING, PROJ_RING, PROD_RING = 8, 8, 8, 2, 3, 8
KEEP_FROM = 1
EARLY_FIRST, EARLY = 6, 4
LATER_FIRST, LATER = 2, 1
W_AHEAD = 6


def with_lo_halves(events, first):
    early, later = (EARLY_FIRST, LATER_FIRST) if first else (EARLY, LATER)
    out, due = [], []
    for ev in events:
        out.append(ev)
        if ev[0] == "T":
            due.append((ev[1], later if ev[1] >= early else 0))
        elif ev[0] in "AB":
            due = [(k, left - 1) for k, left in due]
        out += [("L", k) for k, left in due if left <= 0]
        due = [(k, left) for k, left in due if left > 0]
    return out


def tile_schedule(first):
    group_end = {}
    seen = 0
    for c, chunk in enumerate(CHUNKS):
        if chunk[0] == "twin":
            seen += 1
            if seen % WG == 0:
                group_end[seen // WG - 1] = c // STEP

    def first_step(k):
        return min(c for c, (_, i, _) in enumerate(CHUNKS) if i <= FIELDS - 1 - 2 * k) // STEP

    def arrives(k):
        return 2.9 * (k + 1) + 2.7

    if first:
        ev = [("P", 0), ("T", 0), ("P", 1), ("Q", 0), ("T", 1), ("K", 0), ("Q", 1), ("K", 1), ("P", 2), ("T", 2),
              ("Q", 2), ("K", 2)]
        keep = [3, 4, 5]
    else:
        ev = [("W", g) for g in range(W_AHEAD)]
        ev += [("T", 0), ("R", STEPS - 2), ("R", STEPS - 1), ("Z", ZBANKS - 1), ("T", 1), ("M", 0), ("T", 2), ("M", 1)]
    next_t, next_m, next_w, next_p, begun, clock = 3, 2, W_AHEAD, 3, None, arrives(2) + 1.5
    for t in range(STEPS):
        lowest = min(i for _, i, _ in CHUNKS[STEP * t:STEP * t + STEP])
        needed = (FIELDS - 1 - lowest) // 2
        while next_t < TWINS and (first and (next_t <= needed or clock >= arrives(next_t) and next_t <= needed + 1)
                                  or not first and t >= max(first_step(next_t) - 2, next_t - 2, 1)):
            if next_t == needed:
                clock = max(clock, arrives(next_t) + 2.2)
            ev.append(("T", next_t))
            next_t += 1
        ev.append(("A", t))
        if t >= SLOTS and (t - LAG) % SLOTS == SLOTS - 1:
            ev.append(("Z", t // SLOTS - 1))
        if next_m < MLP:
            ev.append(("M", next_m))
            next_m += 1
        ev.append(("B", t))
        clock += 1
        if not first:
            while next_w < WGROUPS and group_end[next_w - W_AHEAD] <= t:
                ev.append(("W", next_w))
                next_w += 1
        elif begun is not None:
            ev.append(("Q", begun))
            keep += [2 * begun, 2 * begun + 1]
            begun = None
        elif next_p < SPLITS and (2 * next_p < W_RING or group_end[2 * next_p + 1 - W_RING] <= t - 1
                                    and 2 * next_p + 1 - W_RING not in keep):
            ev.append(("P", next_p))
            next_p, begun = next_p + 1, next_p
        if first and keep and t >= KEEP_FROM:
            ev.append(("K", keep.pop(0)))
        if t == MLP:
            ev.append(("D",))
    return with_lo_halves(ev, first)


CHUNK_OF_ODD = {m: c for c, (kind, _, m) in enumerate(CHUNKS) if kind == "odd"}
TWIN_INDEX = {c: n for n, c in enumerate(c for c, x in enumerate(CHUNKS) if x[0] == "twin")}


def last_unit_of_source(i):
    mine = [c for c, (kind, a, m) in enumerate(CHUNKS) if a == i or (kind == "odd" and i == 4 * m + 2)]
    return max(mine) // 2


def last_unit_of_group(g):
    return max(c for c, n in TWIN_INDEX.items() if n // WG == g) // 2


def mov_slot(i):
    return (SOURCES - 1 - i) % MOV_RING


def source_count(i):
    return SOURCES - i


def w_uses(g):
    return len(range(g % W_RING, WGROUPS, W_RING)), g // W_RING + 1


def tower_kernel(nc, ids, tables, dense, w_twin, w_odd, w1, b1, w2, b2, w3, out):
    fp32, f32r, i32 = mybir.dt.float32, mybir.dt.float32r, mybir.dt.int32
    ALU, ACT = mybir.AluOpType, mybir.ActivationFunctionType

    w_split = nc.dram_tensor("w_split", (WGROUPS, P, WCOLS), fp32, kind="Internal").ap()

    with ExitStack() as ctx:
        def sb(name, shape, dt=fp32):
            return ctx.enter_context(nc.sbuf_tensor(name, shape, dt))

        def ps(name, shape):
            return ctx.enter_context(nc.psum_tensor(name, shape, fp32))

        def sem(name):
            return ctx.enter_context(nc.semaphore(name))

        ids_sb = sb("ids_sb", [P, BLOCKS * FIELDS], i32)
        rows = sb("rows", [P, GATHER_RING, BLOCKS, P])
        vT = sb("vT", [P, TWINS, TB])
        v_odd = sb("v_odd", [P, 2, TB])
        mov = sb("mov", [P, MOV_RING, 2, TB], f32r)
        w_raw = sb("w_raw", [P, RAW_RING, WCOLS])
        w_ring = sb("w_ring", [P, W_RING, WCOLS], f32r)
        w_odd_raw = sb("w_odd_raw", [P, ODD, 2, EMBED])
        w_odd_sb = sb("w_odd_sb", [P, ODD, 3, EMBED], f32r)
        prod = sb("prod", [P, PROD_RING, 2, TB])
        sel = sb("sel", [P, SLOTS, 32])
        ident = sb("ident", [P, P])
        z_sb = sb("z_sb", [P, ZBANKS, TB])
        h1_sb = sb("h1_sb", [P, H1 // P, TB])
        h2_sb = sb("h2_sb", [P, H2 // P, TB])
        y_sb = sb("y_sb", [P, TB // 4])
        w1_sb = sb("w1_sb", [P, ZBANKS, H1])
        w2_sb = sb("w2_sb", [P, H1 // P, H2])
        w3_sb = sb("w3_sb", [P, H2 // P])
        b1_sb = sb("b1_sb", [P, H1 // P])
        b2_sb = sb("b2_sb", [P, H2 // P])

        proj = [ps(f"proj{n}", [P, 2, TB]) for n in range(PROJ_RING)]
        z_ps = ps("z_ps", [P, TB])
        desk_ps = ps("desk_ps", [P, TB])

        desks = [proj[PROJ_RING - 1][:, 0, :], proj[PROJ_RING - 1][:, 1, :]] + (MLP - 2) * [desk_ps[:, :]]
        tail_desks = [(desk_ps[:, :], proj[0][:, 0, :])[n % 2] for n in range(MLP)]

        s_passed = sem("waits_passed")
        s_ids = sem("ids_loaded")
        s_rows = [sem(f"rows_gathered{n}") for n in range(GATHER_RING)]
        s_ident = sem("ident_made")
        s_sel = sem("sel_made")
        s_par = sem("parameters_loaded")
        s_oraw = sem("w_odd_loaded")
        s_ohi = sem("w_odd_hi")
        s_olo = sem("w_odd_split")
        s_raw = [sem(f"w_raw_loaded{n}") for n in range(RAW_RING)]
        s_whi = sem("w_hi")
        s_wlo = sem("w_lo")
        s_lomoved = sem("w_lo_moved")
        s_wsp = sem("w_split_done")
        s_scr = [sem(f"w_stored{n}") for n in range(W_RING)]
        s_w = [sem(f"w_loaded{n}") for n in range(W_RING)]
        s_turn = sem("turned")
        s_vt = sem("vt_written")
        s_hi = sem("e_hi")
        s_lo = sem("e_lo")
        s_src_hi = sem("source_hi_ready")
        s_src_lo = sem("source_lo_ready")
        s_vodd = sem("v_odd_copied")
        s_proj = sem("projected")
        s_prod = sem("multiplied")
        s_red = sem("reduced")
        s_z = sem("z_copied")
        s_dense = sem("dense_loaded")
        s_tower = sem("tower_summed")
        s_act = sem("tower_activated")
        s_out = sem("out_stored")

        block = ctx.enter_context(nc.Block())

        def wait(eng, s, tile, per_tile, count):
            value = tile * per_tile + count
            if not isinstance(tile, int) or value > 0:
                eng.wait_ge(s, value)
            if not isinstance(tile, int) and eng in alone:
                eng.sem_inc(s_passed, 1)

        def own(i):
            return slice(i % 2 * EMBED, (i % 2 + 1) * EMBED)

        def other(i):
            return own(i + 1)

        def early(tile):
            return EARLY_FIRST if isinstance(tile, int) else EARLY

        alone = []

        def over_tiles(eng, body):
            body(0)
            with eng.Fori(1, TILES) as tile:
                body(tile)

        @block.gpsimd
        def _(pool):
            alone.append(pool)
            def make_identity():
                pool.memset(ident[:, :], 0.0).then_inc(s_ident, 1)
                pool.wait_ge(s_ident, 1)
                pool.affine_select(out=ident[:, :], in_=ident[:, :], compare_op=ALU.not_equal, fill=1.0,
                                   base=0, pattern=[[-1, P]], channel_multiplier=1).then_inc(s_ident, 1)

            def body(tile):
                for n in range(GATHER_RING):
                    wait(pool, s_rows[n], tile, 2 * 128, 0)
                pool.dma_start(ids_sb[:, :], ids[tile, :, :]).then_inc(s_ids, 16)
                if isinstance(tile, int):
                    make_identity()
                wait(pool, s_ids, tile, 16, 16)
                for k in range(TWINS):
                    wait(pool, s_turn, tile, TWINS, k - GATHER_RING + 1)
                    for blk in range(BLOCKS):
                        for half in range(2):
                            field = 2 * (TWINS - 1 - k) + half
                            at = blk * FIELDS + field
                            pool.indirect_dma_start(
                                rows[:, k % GATHER_RING, blk, half * EMBED:(half + 1) * EMBED], None,
                                tables[field],
                                bass.IndirectOffsetOnAxis(ap=ids_sb[:, at:at + 1], axis=0),
                            ).then_inc(s_rows[k % GATHER_RING], 16)

            over_tiles(pool, body)

        @block.sync
        def _(sp):
            alone.append(sp)
            def load_raw(j):
                if j >= RAW_RING:
                    sp.wait_ge(s_wsp, j - RAW_RING + 1)
                sp.dma_start(w_raw[:, j % RAW_RING, :], w_twin[2 * j:2 * j + 2, :, :]
                             .rearrange("g k c -> (g k) c")).then_inc(s_raw[j % RAW_RING], 16)

            def store_split(g):
                sp.wait_ge(s_wsp, g // 2 + 1)
                sp.dma_start(w_split[g, :, :], w_ring[:, g % W_RING, :].bitcast(fp32)).then_inc(s_scr[g % W_RING], 16)

            def weights(tile, g):
                before = g - W_RING if g >= W_RING else max(range(g % W_RING, WGROUPS, W_RING))
                wait(sp, s_proj, tile, UNITS, last_unit_of_group(before) + 1 - (UNITS if g < W_RING else 0))
                sp.wait_ge(s_scr[g % W_RING], 16 * w_uses(g)[1])
                sp.dma_start(w_ring[:, g % W_RING, :].bitcast(fp32), w_split[g, :, :]).then_inc(s_w[g % W_RING], 16)

            def dense_rows(tile):
                wait(sp, s_tower, tile, MLP, H1 // P - MLP)
                for q in range(4):
                    sp.dma_start(z_sb[32 * q + 28:32 * q + 32, ZBANKS - 1, :],
                                 dense[tile, 4 * q:4 * q + 4, :]).then_inc(s_dense, 16)

            def result(tile):
                wait(sp, s_act, tile, MLP, 1)
                sp.dma_start(out[tile - 1, :, :], y_sb[0:P:32, :]).then_inc(s_out, 16)

            def body(tile):
                first = isinstance(tile, int)
                for ev in tile_schedule(first):
                    if ev[0] == "W" and not first:
                        weights(tile, ev[1])
                    elif ev[0] == "P":
                        for j in (range(RAW_RING) if ev[1] == 0 else ()):
                            load_raw(j)
                    elif ev[0] == "K":
                        store_split(ev[1])
                    elif ev[0] == "Q" and ev[1] + RAW_RING < SPLITS:
                        load_raw(ev[1] + RAW_RING)
                    elif ev[0] == "D":
                        dense_rows(tile)
                    elif ev == ("M", MLP - 1) and not first:
                        result(tile)

            over_tiles(sp, body)
            result(TILES)
            sp.wait_ge(s_out, 16 * TILES + 16)

        @block.scalar
        def _(act):
            for half in range(2):
                act.dma_start(w_odd_raw[half * EMBED:(half + 1) * EMBED, :, :, :], w_odd).then_inc(s_oraw, 16)
            act.sem_inc(s_act, 1)
            act.sem_inc(s_out, 16)
            act.wait_ge(s_oraw, 32)
            act.wait_ge(s_ohi, 1)
            act.activation(w_odd_sb[:, :, 0:3:2, :], w_odd_raw[:, :, :, :], ACT.Copy).then_inc(s_ohi, 1)

            def load_parameters():
                act.dma_start(w1_sb[:, :, :], w1).then_inc(s_par, 16)
                act.dma_start(w2_sb[:, :, :], w2).then_inc(s_par, 16)
                act.dma_start(w3_sb[:, :], w3).then_inc(s_par, 16)
                act.dma_start(b1_sb[:, :], b1).then_inc(s_par, 16)
                act.dma_start(b2_sb[:, :], b2).then_inc(s_par, 16)

            def weights_hi(j):
                even, odd = 2 * j, 2 * j + 1
                act.wait_ge(s_raw[j % RAW_RING], 16 * (j // RAW_RING + 1))
                if even >= W_RING:
                    act.wait_ge(s_proj, last_unit_of_group(odd - W_RING) + 1)
                    for g in (even, odd):
                        act.wait_ge(s_scr[g % W_RING], 16 * (g // W_RING))
                act.activation(w_ring[:, even % W_RING, :], w_raw[:, j % RAW_RING, :], ACT.Copy).then_inc(s_whi, 1)

            def weights_placed(j):
                even, odd = 2 * j % W_RING, (2 * j + 1) % W_RING
                act.wait_ge(s_wlo, j + 1)
                act.activation(w_ring[EMBED:P, even, :], w_ring[0:EMBED, odd, :].bitcast(fp32),
                               ACT.Copy).then_inc(s_lomoved, 1)
                act.wait_ge(s_lomoved, j + 1)
                act.activation(w_ring[0:EMBED, odd, :], w_raw[EMBED:P, j % RAW_RING, :], ACT.Copy).then_inc(s_wsp, 1)

            def turned(tile, k):
                m = TWINS - 1 - k
                mine = [i for i in (2 * m + 1, 2 * m) if i < SOURCES]
                wait(act, s_turn, tile, TWINS, k + 1)
                if k == 0:
                    wait(act, s_prod, tile, UNITS, 0)
                act.activation(vT[:, m, :], desk_ps[:, :], ACT.Copy).then_inc(s_vt, 1)
                for i in mine:
                    before = i + MOV_RING
                    if before < SOURCES:
                        wait(act, s_proj, tile, UNITS, last_unit_of_source(before) + 1)
                    else:
                        before = min(x for x in range(SOURCES) if mov_slot(x) == mov_slot(i))
                        wait(act, s_proj, tile, UNITS, last_unit_of_source(before) + 1 - UNITS)
                wait(act, s_vt, tile, TWINS, k + 1)
                for i in mine:
                    last = act.activation(mov[own(i), mov_slot(i), 0, :], vT[own(i), m, :], ACT.Copy)
                last.then_inc(s_hi, 1)
                wait(act, s_hi, tile, TWINS, k + 1)
                for i in mine:
                    act.activation(mov[other(i), mov_slot(i), 0, :], mov[own(i), mov_slot(i), 0, :].bitcast(fp32),
                                   ACT.Copy).then_inc(s_src_hi, 1)
                if m % 2 == 0:
                    g = m // 2
                    if g + 2 < ODD:
                        wait(act, s_prod, tile, UNITS, CHUNK_OF_ODD[g + 2] // 2 + 1)
                    else:
                        wait(act, s_prod, tile, UNITS, CHUNK_OF_ODD[g % 2] // 2 + 1 - UNITS)
                    act.activation(v_odd[0:EMBED, g % 2, :], vT[EMBED:P, m, :], ACT.Copy)
                    act.activation(v_odd[EMBED:P, g % 2, :], vT[EMBED:P, m + 1, :], ACT.Copy).then_inc(s_vodd, 1)
                for i in mine if k >= early(tile) else ():
                    wait(act, s_lo, tile, SOURCES, source_count(i))
                    act.activation(mov[other(i), mov_slot(i), 1, :], mov[own(i), mov_slot(i), 1, :].bitcast(fp32),
                                   ACT.Copy).then_inc(s_src_lo, 1)

            def tower(tile, n, banks):
                mlp_ps = banks[n]
                wait(act, s_tower, tile, MLP, n + 1 - MLP)
                if n < H1 // P:
                    act.activation(h1_sb[:, n, :], mlp_ps, ACT.Relu,
                                   bias=b1_sb[:, n:n + 1]).then_inc(s_act, 1)
                elif n < MLP - 1:
                    c = n - H1 // P
                    act.activation(h2_sb[:, c, :], mlp_ps, ACT.Relu,
                                   bias=b2_sb[:, c:c + 1]).then_inc(s_act, 1)
                else:
                    wait(act, s_out, tile, 16, 0)
                    act.activation(y_sb[:, :], mlp_ps[:, 0:TB // 4], ACT.Copy).then_inc(s_act, 1)

            def z_copy(tile, G):
                wait(act, s_red, tile, STEPS, SLOTS * (G + 1) if G < ZBANKS - 1 else 0)
                if G < ZBANKS - 1:
                    act.activation(z_sb[:, G, :], z_ps[:, :], ACT.Copy).then_inc(s_z, 1)
                    return
                for q in range(4):
                    part = slice(32 * q, 32 * q + 28)
                    last = act.activation(z_sb[part, G, :], z_ps[part, :], ACT.Copy)
                last.then_inc(s_z, 1)

            def body(tile):
                first = isinstance(tile, int)
                for ev in tile_schedule(first):
                    if ev[0] == "P":
                        weights_hi(ev[1])
                    elif ev[0] == "Q":
                        weights_placed(ev[1])
                    elif ev[0] == "T":
                        turned(tile, ev[1])
                        if first and ev[1] == TWINS - 1:
                            load_parameters()
                    elif ev[0] == "M" and not first:
                        tower(tile, ev[1], desks)
                    elif ev[0] == "Z" and not (first and ev[1] == ZBANKS - 1):
                        z_copy(tile, ev[1])
                if first:
                    act.wait_ge(s_par, 80)

            over_tiles(act, body)
            z_copy(TILES, ZBANKS - 1)
            for n in range(MLP):
                tower(TILES, n, tail_desks)

        @block.vector
        def _(dve):
            dve.memset(w_odd_sb[:, :, :, :].bitcast(fp32), 0.0).then_inc(s_ohi, 1)
            dve.memset(sel[:, :, :], 0.0).then_inc(s_sel, 1)
            dve.wait_ge(s_sel, 1)
            flat = sel[:, :, :].rearrange("p s c -> p (s c)")
            for half in range(2):
                last = 34 * (SLOTS - 1) + half
                dve.memset(flat[half * EMBED:(half + 1) * EMBED, half:last + 1:34], 1.0).then_inc(s_sel, 1)
            dve.wait_ge(s_ohi, 2)
            dve.tensor_tensor(w_odd_sb[EMBED:P, :, 0:3:2, :], w_odd_raw[EMBED:P, :, :, :],
                              w_odd_sb[EMBED:P, :, 0:3:2, :].bitcast(fp32), ALU.subtract).then_inc(s_olo, 1)

            def weights_lo(j):
                dve.wait_ge(s_whi, j + 1)
                dve.tensor_tensor(w_ring[:, (2 * j + 1) % W_RING, :], w_raw[:, j % RAW_RING, :],
                                  w_ring[:, 2 * j % W_RING, :].bitcast(fp32), ALU.subtract).then_inc(s_wlo, 1)

            def lo(tile, k):
                m = TWINS - 1 - k
                wait(dve, s_vt, tile, TWINS, k + 1)
                wait(dve, s_hi, tile, TWINS, k + 1)
                for i in (2 * m + 1, 2 * m):
                    if i < SOURCES:
                        dve.tensor_tensor(mov[own(i), mov_slot(i), 1, :], vT[own(i), m, :],
                                          mov[own(i), mov_slot(i), 0, :].bitcast(fp32), ALU.subtract).then_inc(s_lo, 1)
                    if i < SOURCES and k < early(tile):
                        dve.tensor_tensor(mov[other(i), mov_slot(i), 1, :], vT[own(i), m, :],
                                          mov[own(i), mov_slot(i), 0, :].bitcast(fp32),
                                          ALU.subtract).then_inc(s_src_lo, 1)

            def multiply(tile, u):
                a, b = CHUNKS[2 * u], CHUNKS[2 * u + 1]
                wait(dve, s_proj, tile, UNITS, u + 1)
                before = u - PROD_RING if u >= PROD_RING else max(range(u, UNITS, PROD_RING)) - UNITS
                wait(dve, s_red, tile, STEPS, before // 2 + 1)
                if a[0] == b[0] == "twin" and a[2] < b[2]:
                    dve.tensor_tensor(prod[:, u % PROD_RING, :, :], proj[u % PROJ_RING][:, :, :],
                                      vT[:, a[2]:b[2] + 1:b[2] - a[2], :], ALU.mult).then_inc(s_prod, 1)
                    return
                for n, (kind, _, m) in enumerate((a, b)):
                    if kind == "odd":
                        wait(dve, s_vodd, tile, ODD, ODD - m)
                    target = vT[:, m, :] if kind == "twin" else v_odd[:, m % 2, :]
                    last = dve.tensor_tensor(prod[:, u % PROD_RING, n, :], proj[u % PROJ_RING][:, n, :], target, ALU.mult)
                last.then_inc(s_prod, 1)

            def body(tile):
                first = isinstance(tile, int)
                for ev in tile_schedule(first):
                    if ev[0] == "P":
                        weights_lo(ev[1])
                    elif ev[0] == "L":
                        lo(tile, ev[1])
                    elif ev[0] in "AB":
                        multiply(tile, 2 * ev[1] + (ev[0] == "B"))

            over_tiles(dve, body)

        @block.tensor
        def _(pe):
            pe.wait_ge(s_ident, 2)
            pe.wait_ge(s_sel, 3)
            pe.wait_ge(s_olo, 1)

            def turn(tile, k):
                wait(pe, s_rows[k % GATHER_RING], tile, 2 * 128, 128 * (k // GATHER_RING + 1))
                wait(pe, s_vt, tile, TWINS, k)
                for blk in range(BLOCKS):
                    last = pe.transpose(desk_ps[:, blk * P:(blk + 1) * P],
                                        rows[:, k % GATHER_RING, blk, :], ident[:, :])
                last.then_inc(s_turn, 1)

            def weights_ready(tile, g):
                if isinstance(tile, int):
                    pe.wait_ge(s_wsp, g // 2 + 1)
                else:
                    per, use = w_uses(g)
                    wait(pe, s_w[g % W_RING], tile, 16 * per, 16 * (use - per))

            def source_ready(tile, i):
                wait(pe, s_src_hi, tile, SOURCES, source_count(i))
                wait(pe, s_src_lo, tile, SOURCES, source_count(i))

            def project(tile, u):
                before = u - PROJ_RING if u >= PROJ_RING else max(range(u, UNITS, PROJ_RING)) - UNITS
                wait(pe, s_prod, tile, UNITS, before + 1)
                if u == PROJ_RING - 1 and not isinstance(tile, int):
                    wait(pe, s_act, tile, MLP, 3 - MLP)
                for n in range(2):
                    c = 2 * u + n
                    kind, i, m = CHUNKS[c]
                    if kind == "twin":
                        w = TWIN_INDEX[c]
                        if w % WG == 0:
                            weights_ready(tile, w // WG)
                        if m == i // 2 + 1:
                            source_ready(tile, i)
                        wt = w_ring[:, (w // WG) % W_RING, (w % WG) * P:(w % WG + 1) * P]
                        parts = [(wt, i)]
                    else:
                        if m == ODD - 1:
                            source_ready(tile, i + 2)
                        wo = w_odd_sb[:, m, :, :].rearrange("p a l -> p (a l)")
                        parts = [(wo[:, 0:P], i), (wo[:, EMBED:EMBED + P], i + 2)]
                    passes = [(wt, src, part) for wt, src in parts for part in range(2)]
                    for x, (wt, src, part) in enumerate(passes):
                        last = pe.matmul(proj[u % PROJ_RING][:, n, :], lhsT=wt, rhs=mov[:, mov_slot(src), part, :],
                                         start=(x == 0), stop=(x == len(passes) - 1))
                last.then_inc(s_proj, 1)

            def reduce(tile, t, ago=0):
                bank, slot = t // SLOTS, t % SLOTS
                wait(pe, s_prod, tile, UNITS, 2 * t + 2 - ago * UNITS)
                if slot == 0:
                    wait(pe, s_z, tile, ZBANKS, bank)
                for q in range(STEP):
                    last = pe.matmul(z_ps[32 * q:32 * q + 32, :], lhsT=sel[:, slot, :],
                                     rhs=prod[:, (2 * t + q // 2) % PROD_RING, q % 2, :],
                                     start=(slot == 0), stop=(slot == SLOTS - 1 or t == STEPS - 1))
                last.then_inc(s_red, 1)

            def tower(tile, n, banks):
                mlp_ps = banks[n]
                tail = banks is tail_desks
                if tail:
                    wait(pe, s_act, tile, MLP, n + (n == MLP - 1) - MLP)
                elif n == 0 or n >= 3:
                    wait(pe, s_act, tile, MLP, n + 1 - MLP)
                if n == 0:
                    pe.wait_ge(s_par, 80)
                    wait(pe, s_z, tile, ZBANKS, -1)
                if n < H1 // P:
                    for G in range(ZBANKS):
                        if n == 0 and G == ZBANKS - 1:
                            wait(pe, s_z, tile, ZBANKS, 0)
                            wait(pe, s_dense, tile, 64, 0)
                        last = pe.matmul(mlp_ps, lhsT=w1_sb[:, G, n * P:(n + 1) * P], rhs=z_sb[:, G, :],
                                         start=(G == 0), stop=(G == ZBANKS - 1))
                elif n < MLP - 1:
                    c = n - H1 // P
                    for G in range(H1 // P):
                        if tail and c == 0:
                            wait(pe, s_act, tile, MLP, G + 2 - MLP)
                        last = pe.matmul(mlp_ps, lhsT=w2_sb[:, G, c * P:(c + 1) * P], rhs=h1_sb[:, G, :],
                                         start=(G == 0), stop=(G == H1 // P - 1))
                else:
                    for G in range(H2 // P):
                        for q in range(4):
                            last = pe.matmul(mlp_ps[32 * q:32 * q + 1, 0:TB // 4], lhsT=w3_sb[:, G:G + 1],
                                             rhs=h2_sb[:, G, q * TB // 4:(q + 1) * TB // 4],
                                             start=(G == 0), stop=(G == H2 // P - 1))
                last.then_inc(s_tower, 1)

            def body(tile):
                first = isinstance(tile, int)
                turns = items = 0
                for ev in tile_schedule(first):
                    if ev[0] == "T":
                        if items > 2 and not first:
                            wait(pe, s_act, tile, MLP, items + 1 - MLP)
                        turn(tile, ev[1])
                        turns += 1
                    elif ev[0] == "M" and not first:
                        if items >= 2:
                            wait(pe, s_vt, tile, TWINS, turns)
                        tower(tile, ev[1], desks)
                        items += 1
                    elif ev[0] == "A":
                        project(tile, 2 * ev[1])
                        if ev[1] > LAG and (ev[1] - LAG) % 2:
                            reduce(tile, ev[1] - LAG - 1)
                            reduce(tile, ev[1] - LAG)
                    elif ev[0] == "B":
                        project(tile, 2 * ev[1] + 1)
                    elif ev[0] == "R" and not first:
                        reduce(tile, ev[1], ago=1)

            over_tiles(pe, body)
            for t in range(STEPS - LAG, STEPS):
                reduce(TILES, t, ago=1)
            for n in range(MLP):
                tower(TILES, n, tail_desks)


def kernel(**inputs):
    import concourse.bacc as bacc
    from concourse.bass_utils import run_bass_kernel_spmd

    a = {k: np.asarray(v) for k, v in inputs.items()}
    twin_rows = np.array([[pair_row(*p) for p in chunk_pairs(c)] for c in TWIN_CHUNKS])
    odd_rows = np.array([[pair_row(*p) for p in chunk_pairs(CHUNKS[CHUNK_OF_ODD[g]])] for g in range(ODD)])
    z_rows = np.zeros(ZBANKS * P, np.int64)
    for c, chunk in enumerate(CHUNKS):
        for half, p in enumerate(chunk_pairs(chunk)):
            z_rows[z_row(c, half)] = pair_row(*p)
    for d in range(DENSE):
        z_rows[dense_row(d)] = FIELDS * (FIELDS - 1) // 2 + d

    w = a["L0_rec_w"]
    arrays = {
        "ids": a["ids"].reshape(TILES, BLOCKS, P, FIELDS).transpose(0, 2, 1, 3).reshape(TILES, P, BLOCKS * FIELDS),
        "dense": a["dense_ctx"].reshape(TILES, TB, DENSE).transpose(0, 2, 1),
        "w_twin": w[twin_rows].reshape(WGROUPS, WG, 2, EMBED, EMBED).transpose(0, 3, 1, 2, 4)
                  .reshape(WGROUPS, EMBED, WCOLS),
        "w_odd": w[odd_rows].transpose(2, 0, 1, 3),
        "w1": a["W_top1"][z_rows].reshape(ZBANKS, P, H1).transpose(1, 0, 2),
        "b1": a["b_top1"].reshape(H1 // P, P).T,
        "w2": a["W_top2"].reshape(H1 // P, P, H2).transpose(1, 0, 2),
        "b2": a["b_top2"].reshape(H2 // P, P).T,
        "w3": a["W_top3"].reshape(H2 // P, P).T,
    }
    arrays |= {f"tbl_{f}": a[f"tbl_{f}"] for f in range(FIELDS)}
    arrays = {k: np.ascontiguousarray(v) for k, v in arrays.items()}

    nc = bacc.Bacc("TRN2", target_bir_lowering=False, num_devices=1)
    ap = {k: nc.dram_tensor(k, v.shape, mybir.dt.from_np(v.dtype), kind="ExternalInput").ap()
          for k, v in arrays.items()}
    out = nc.dram_tensor("out", (TILES, 4, TB // 4), mybir.dt.float32, kind="ExternalOutput").ap()
    tower_kernel(nc, ap["ids"], [ap[f"tbl_{f}"] for f in range(FIELDS)], ap["dense"], ap["w_twin"], ap["w_odd"],
                 ap["w1"], ap["b1"], ap["w2"], ap["b2"], ap["w3"], out)
    r = run_bass_kernel_spmd(nc, [arrays], core_ids=[0])
    return r.results[0]["out"].reshape(BATCH, 1)
```
